# Optimizing a Trainium2 kernel written in Bass

```python
import numpy as np
import jax
import jax.numpy as jnp

def _softmax(x, axis=-1):
    return jax.nn.softmax(x, axis=axis)
def _gelu(x):
    return jax.nn.gelu(x, approximate=True)
def _silu(x):
    return jax.nn.silu(x)
def _sigmoid(x):
    return jax.nn.sigmoid(x)
def _layernorm(x, axis=-1, eps=1e-5):
    m = jnp.mean(x, axis=axis, keepdims=True)
    v = jnp.var(x, axis=axis, keepdims=True)
    return (x - m) / jnp.sqrt(v + eps)
def _scatter_add(tgt, idx, src, axis=0):
    return tgt.at[idx].add(src)
def _segment_sum(src, seg, n):
    return jax.ops.segment_sum(src, seg, n)

kernel_name = 'mk_adj_preln_d2_adj_512_130db9'

def setup_inputs(seed: int = 0):
    np.random.seed(seed)
    _w = jnp.asarray
    def _rec_inputs():
        import jax
        import jax.numpy as jnp
        _gk = jax.random.key(seed)
        x = 7.22e-05 + 1 * jax.random.normal(jax.random.fold_in(_gk, 1), (64, 256, 512), jnp.float32)
        _a = jax.random.bernoulli(jax.random.fold_in(_gk, 2), 0.125, (64, 256, 256))
        _a = jnp.logical_or(_a, jnp.swapaxes(_a, -1, -2))
        _a = jnp.logical_or(_a, jnp.eye(256, dtype=bool))
        _af = _a.astype(jnp.float32)
        _af = _af * jax.random.uniform(jax.random.fold_in(_gk, 3), (64, 256, 256), jnp.float32, 0.05, 1)
        adj = _af
        return x, adj
    x, adj = _rec_inputs()
    def _L0_gnn_setup():
        import jax, jax.numpy as jnp
        import numpy as np
        B, N, D = (8, 2048, 512)
        key = jax.random.key(seed)
        ks = jax.random.split(key, 8)
        scale = 0.5 / np.sqrt(D)
        x = jax.random.normal(ks[0], (B, N, D), dtype=jnp.float32)
        adj = jax.random.uniform(ks[1], (B, N, N), dtype=jnp.float32)
        Wq_w = jax.random.normal(ks[2], (D, D), dtype=jnp.float32) * scale
        Wk_w = jax.random.normal(ks[3], (D, D), dtype=jnp.float32) * scale
        Wv_w = jax.random.normal(ks[4], (D, D), dtype=jnp.float32) * scale
        Wq_b = jnp.zeros((D,), dtype=jnp.float32)
        Wk_b = jnp.zeros((D,), dtype=jnp.float32)
        Wv_b = jnp.zeros((D,), dtype=jnp.float32)
        return {'x': x, 'adj': adj, 'Wq_w': Wq_w, 'Wq_b': Wq_b, 'Wk_w': Wk_w, 'Wk_b': Wk_b, 'Wv_w': Wv_w, 'Wv_b': Wv_b}
    _L0_gnn_all = _L0_gnn_setup()
    _L0_gnn_in = {k: v for k, v in _L0_gnn_all.items() if k in ('Wq_w', 'Wq_b', 'Wk_w', 'Wk_b', 'Wv_w', 'Wv_b', )}
    del _L0_gnn_all

    def _L1_gnn_setup():
        import jax, jax.numpy as jnp
        import numpy as np
        EPS = 1e-06
        key = jax.random.key(seed)
        k1, k2, k3 = jax.random.split(key, 3)
        B, N, F, O = (8, 4096, 512, 512)
        x = jax.random.normal(k1, (B, N, F), dtype=jnp.float32)
        adj = jax.random.uniform(k2, (B, N, N), dtype=jnp.float32)
        W = jax.random.normal(k3, (O, 2 * F), dtype=jnp.float32) * (1.0 / np.sqrt(2 * F))
        return {'x': x, 'adj': adj, 'W': W}
    _L1_gnn_all = _L1_gnn_setup()
    _L1_gnn_in = {k: v for k, v in _L1_gnn_all.items() if k in ('W', )}
    del _L1_gnn_all

    return {
        "x": x,
        "adj": adj,
        "L0_gnn_Wq_w": _L0_gnn_in["Wq_w"],
        "L0_gnn_Wq_b": _L0_gnn_in["Wq_b"],
        "L0_gnn_Wk_w": _L0_gnn_in["Wk_w"],
        "L0_gnn_Wk_b": _L0_gnn_in["Wk_b"],
        "L0_gnn_Wv_w": _L0_gnn_in["Wv_w"],
        "L0_gnn_Wv_b": _L0_gnn_in["Wv_b"],
        "L1_gnn_W": _L1_gnn_in["W"],
    }

def reference(x, adj, L0_gnn_Wq_w, L0_gnn_Wq_b, L0_gnn_Wk_w, L0_gnn_Wk_b, L0_gnn_Wv_w, L0_gnn_Wv_b, L1_gnn_W):
    import jax
    import jax.numpy as jnp
    def _L0_gnn_ref(x, adj, Wq_w, Wq_b, Wk_w, Wk_b, Wv_w, Wv_b):
        import jax, jax.numpy as jnp
        import numpy as np
        B, N, D = (8, 2048, 512)
        query = jnp.einsum('bnd,od->bno', x, Wq_w) + Wq_b
        keyt = jnp.einsum('bnd,od->bno', x, Wk_w) + Wk_b
        value = jnp.einsum('bnd,od->bno', x, Wv_w) + Wv_b
        weight = jnp.einsum('bqd,bkd->bqk', query, keyt)
        weight = adj * jnp.exp(weight)
        weight = weight / jnp.sum(weight, axis=2, keepdims=True)
        return jnp.einsum('bqk,bkd->bqd', weight, value)

    def _L1_gnn_ref(x, adj, W):
        import jax, jax.numpy as jnp
        import numpy as np
        EPS = 1e-06
        deg = jnp.sum(adj, axis=-1, keepdims=True)
        agg = jnp.einsum('bij,bjf->bif', adj, x) / jnp.maximum(deg, EPS)
        cat = jnp.concatenate([x, agg], axis=2)
        out = jnp.einsum('bnf,of->bno', cat, W)
        return jax.nn.relu(out)

    h = jnp.maximum(_layernorm(x, axis=-1), 0.0)
    x = x + _L0_gnn_ref(h, adj, L0_gnn_Wq_w, L0_gnn_Wq_b, L0_gnn_Wk_w, L0_gnn_Wk_b, L0_gnn_Wv_w, L0_gnn_Wv_b)
    h = jnp.maximum(_layernorm(x, axis=-1), 0.0)
    x = x + _L1_gnn_ref(h, adj, L1_gnn_W)
    return x


_drawn_inputs = setup_inputs


def setup_inputs(seed=0):
    import zlib

    import numpy as np

    out = dict(_drawn_inputs(seed))
    spreads = {'L0_gnn_Wq_b': (0.0, 0.1), 'L0_gnn_Wk_b': (0.0, 0.1), 'L0_gnn_Wv_b': (0.0, 0.1)}
    factors = {}
    for name, (base, spread) in spreads.items():
        noise = np.random.default_rng([zlib.crc32(name.encode()), seed]).standard_normal(out[name].shape)
        drawn = base * np.exp(spread * noise) if base else spread * noise
        out[name] = jnp.asarray(drawn.astype(out[name].dtype))
    for name, factor in factors.items():
        out[name] = (out[name] * factor).astype(out[name].dtype)
    return out
```

```python
from contextlib import ExitStack

import concourse.bass as bass
from concourse import mybir

F32 = mybir.dt.float32
F32R = mybir.dt.float32r
ALU = mybir.AluOpType
ACT = mybir.ActivationFunctionType
AX_X = mybir.AxisListType.X

P = 128
LN_EPS = 1e-5
DEG_EPS = 1e-6
L0_BANK, L1_BANK, TR_BANK = 0, 4, 6


def gnn_layers(nc, x, adj, wq, bq, wk, bk, wv_t, bv, w1_t, out):
    graphs, nodes, dim = x.shape
    G = 2
    PAIRS = graphs // G
    NT = nodes // P
    T = G * NT
    DT = dim // P
    N = T * P
    assert graphs % G == 0 and PAIRS >= 4 and NT == 2 and T == 4 and DT == 4 and dim == 512

    x_d = x.rearrange("(i g) (t p) d -> i p (g t) d", g=G, p=P)
    adj_d = adj.rearrange("(i g) (t p) j -> i p (g t) j", g=G, p=P)
    out_d = out.rearrange("(i g) (t p) d -> i (g t) p d", g=G, p=P)

    with ExitStack() as ctx:
        def sb(name, shape, dt=F32):
            return ctx.enter_context(nc.sbuf_tensor(name, shape, dt))

        def sem(name):
            return ctx.enter_context(nc.semaphore(name))

        n_h, n_l = sb("n_h", [P, DT, dim], F32R), sb("n_l", [P, DT, dim], F32R)
        wv_h, wv_l = sb("wv_h", [P, DT, dim], F32R), sb("wv_l", [P, DT, dim], F32R)
        wa_h, wa_l = sb("wa_h", [P, DT, dim], F32R), sb("wa_l", [P, DT, dim], F32R)
        wb_h, wb_l = sb("wb_h", [P, DT, dim], F32R), sb("wb_l", [P, DT, dim], F32R)
        hT_h, hT_l = sb("hT_h", [P, DT, N], F32R), sb("hT_l", [P, DT, N], F32R)
        gT_h, gT_l = sb("gT_h", [P, DT, N], F32R), sb("gT_l", [P, DT, N], F32R)
        kz_h, kz_l = sb("kz_h", [P, 4, 512], F32R), sb("kz_l", [P, 4, 512], F32R)
        v_h, v_l = sb("v_h", [P, T, dim], F32R), sb("v_l", [P, T, dim], F32R)
        w_h, w_l = sb("w_h", [P, G, NT, nodes], F32R), sb("w_l", [P, G, NT, nodes], F32R)
        at_h, at_l = sb("at_h", [P, G, NT, nodes], F32R), sb("at_l", [P, G, NT, nodes], F32R)
        x_in = sb("x_in", [P, T, dim])
        xb = sb("xb", [P, T, dim])
        x1 = sb("x1", [P, T, dim])
        h = sb("h", [P, T, dim])
        x2 = sb("x2", [P, 2, dim])
        adj_in = sb("adj_in", [P, T, nodes])
        adjT = sb("adjT", [P, G, NT, nodes])
        w_sum = sb("w_sum", [P, G, nodes])
        w = sb("w", [P, G, NT, nodes])
        bq_b = w[:, :, :, :].rearrange("p g t n -> p (g t n)")
        ident = sb("ident", [P, P])
        ones = sb("ones", [P, 1])
        minus_half = sb("minus_half", [P, NT])
        bv_b = sb("bv_b", [P, dim])
        u_b = sb("u_b", [P, dim])
        scratch = sb("scratch", [P, dim])
        bq_c, bk_c = sb("bq_c", [P, DT]), sb("bk_c", [P, DT])
        kp_bias = sb("kp_bias", [P, DT])
        bqk = sb("bqk", [P, 1])
        key_bias = sb("key_bias", [P, T])
        stats = [sb(f"stats{n}", [P, T, 6]) for n in range(2)]
        mean_var = [sb(f"mean_var{n}", [P, T, 2]) for n in range(2)]
        var_eps = [sb(f"var_eps{n}", [P, T]) for n in range(2)]
        mean_sum = [sb(f"mean_sum{n}", [P, T]) for n in range(2)]
        rstd = [sb(f"rstd{n}", [P, T]) for n in range(2)]
        half_rstd = [sb(f"half_rstd{n}", [P, T]) for n in range(2)]
        shift = [sb(f"shift{n}", [P, T]) for n in range(2)]
        deg, deg_max, deg_inv = sb("deg", [P, T]), sb("deg_max", [P, T]), sb("deg_inv", [P, T])
        sum_inv = sb("sum_inv", [P, T])

        bank = [ctx.enter_context(nc.psum_tensor(f"bank{b}", [P, 512], F32)) for b in range(8)]

        wqk_loaded, bias_loaded = sem("wqk_loaded"), sem("bias_loaded")
        weight_loaded = [sem(f"{name}_loaded") for name in ("wv", "wa", "wb")]
        consts, ident_zero, ident_done = sem("consts"), sem("ident_zero"), sem("ident_done")
        bq_spread, setup_psum = sem("bq_spread"), sem("setup_psum")
        n_high, n_split, setup_small = sem("n_high"), sem("n_split"), sem("setup_small")
        weight_high, weight_split = sem("weight_high"), sem("weight_split")
        x_loaded, adj_loaded = sem("x_loaded"), sem("adj_loaded")
        out_stored = [sem(f"out_stored{k}") for k in range(2)]
        stats_done = [sem(f"stats_done{n}") for n in range(2)]
        aggr_done = [sem(f"aggr_done{n}") for n in range(2)]
        moments_done = [sem(f"moments_done{n}") for n in range(2)]
        rstd_done = [sem(f"rstd_done{n}") for n in range(2)]
        shift_done = [sem(f"shift_done{n}") for n in range(2)]
        h_done = [sem(f"h_done{n}") for n in range(2)]
        key_bias_done, xb_done = sem("key_bias_done"), sem("xb_done")
        deg_done, adj_scaled = sem("deg_done"), sem("adj_scaled")
        hT_psum, hT_high, hT_split = sem("hT_psum"), sem("hT_high"), sem("hT_split")
        gT_psum, gT_high, gT_split = sem("gT_psum"), sem("gT_high"), sem("gT_split")
        at_psum, at_copied, at_high, at_split = sem("at_psum"), sem("at_copied"), sem("at_high"), sem("at_split")
        kp_psum, kp_high, kp_split = sem("kp_psum"), sem("kp_high"), sem("kp_split")
        v_psum, v_high, v_split = sem("v_psum"), sem("v_high"), sem("v_split")
        z_psum, z_high, z_split = sem("z_psum"), sem("z_high"), sem("z_split")
        score_psum, exp_done = sem("score_psum"), sem("exp_done")
        w_done, w_high, w_split, w_summed = sem("w_done"), sem("w_high"), sem("w_split"), sem("w_summed")
        sum_psum, sum_inv_done = sem("sum_psum"), sem("sum_inv_done")
        av_psum, x1_done = sem("av_psum"), sem("x1_done")
        l1_psum, x2_done = sem("l1_psum"), sem("x2_done")

        def steps(engine, step):
            step(0, layer1=False)
            step(1)
            with engine.Fori(2, PAIRS - 1) as i:
                step(i)
            step(PAIRS - 1, more=False)
            step(PAIRS, layer0=False, more=False)

        block = ctx.enter_context(nc.Block())

        @block.sync
        def _(sp):
            def load_x(i):
                sp.dma_start(x_in[:, :, :], x_d[i]).then_inc(x_loaded, 16)

            def load_adj(i):
                sp.dma_start(adj_in[:, :, :], adj_d[i]).then_inc(adj_loaded, 16)

            def load_weight(n):
                src = (wv_t, w1_t[0:dim], w1_t[dim:2 * dim])[n]
                if n:
                    sp.wait_ge(weight_split, n)
                sp.dma_start(x1[:, :, :], src.rearrange("(t p) o -> p t o", p=P)).then_inc(weight_loaded[n], 16)

            sp.dma_start(x1[:, :, :], wq.rearrange("(t p) d -> p t d", p=P)).then_inc(wqk_loaded, 16)
            sp.dma_start(xb[:, :, :], wk.rearrange("(t p) d -> p t d", p=P)).then_inc(wqk_loaded, 16)
            load_x(0)
            sp.dma_start(bq_c[:, :], bq.rearrange("(t p) -> p t", p=P),
                         allow_slow_non_contiguous=True).then_inc(bias_loaded, 16)
            sp.dma_start(bk_c[:, :], bk.rearrange("(t p) -> p t", p=P),
                         allow_slow_non_contiguous=True).then_inc(bias_loaded, 16)
            sp.dma_start(bv_b[:, :], bv.rearrange("(a d) -> a d", a=1).to_broadcast([P, dim])).then_inc(bias_loaded, 16)
            load_adj(0)
            sp.wait_ge(setup_psum, DT + 2)
            load_weight(0)
            load_weight(1)

            def step(i, layer0=True, layer1=True, more=True):
                if more:
                    sp.wait_ge(xb_done, T * (i + 1))
                    load_x(i + 1)
                    sp.wait_ge(at_psum, G * (i + 1))
                    load_adj(i + 1)
                if layer0 and not layer1:
                    load_weight(2)
                if layer1:
                    j = i - 1
                    for t in range(T):
                        sp.wait_ge(x2_done, T * j + t + 1)
                        sp.dma_start(out_d[j, t], x2[:, t % 2, :]).then_inc(out_stored[t % 2], 16)

            steps(sp, step)
            for k in range(2):
                sp.wait_ge(out_stored[k], 16 * PAIRS * T // 2)

        @block.gpsimd
        def _(pool):
            pool.memset(minus_half[:, :], -0.5).then_inc(consts, 1)
            pool.memset(scratch[:, :], 1.0).then_inc(consts, 1)
            pool.memset(ident[:, :], 0.0).then_inc(ident_zero, 1)
            pool.wait_ge(ident_zero, 1)
            pool.affine_select(out=ident[:, :], in_=ident[:, :], compare_op=ALU.not_equal, fill=1.0,
                               base=0, pattern=[[-1, P]], channel_multiplier=1).then_inc(ident_done, 1)

            def scale_and_shift(n, i):
                for g in range(G):
                    tiles = slice(NT * g, NT * g + NT)
                    pool.wait_ge(moments_done[n], 2 * (G * i + g + 1))
                    pool.tensor_tensor(rstd[n][:, tiles], var_eps[n][:, tiles], minus_half[:, :],
                                       ALU.pow).then_inc(rstd_done[n], 1)
                    pool.wait_ge(rstd_done[n], 2 * (G * i + g) + 1)
                    pool.tensor_tensor(half_rstd[n][:, tiles], rstd[n][:, tiles], minus_half[:, :],
                                       ALU.mult).then_inc(rstd_done[n], 1)
                    pool.wait_ge(rstd_done[n], 2 * (G * i + g) + 2)
                    pool.tensor_tensor(shift[n][:, tiles], mean_sum[n][:, tiles], half_rstd[n][:, tiles],
                                       ALU.mult).then_inc(shift_done[n], 1)

            def add_bv(i):
                pool.wait_ge(x_loaded, 16 * (i + 1))
                for t in range(T):
                    pool.tensor_tensor(xb[:, t, :], x_in[:, t, :], bv_b[:, :], ALU.add).then_inc(xb_done, 1)

            pool.wait_ge(consts, 2)
            scale_and_shift(0, 0)
            pool.wait_ge(bias_loaded, 48)
            pool.wait_ge(setup_psum, DT + 2)

            def step(i, layer0=True, layer1=True, more=True):
                if layer1:
                    scale_and_shift(1, i - 1)
                if not layer0:
                    return
                if layer1:
                    pool.wait_ge(x1_done, T * i)
                add_bv(i)
                for g in range(G):
                    pool.wait_ge(w_high, G * i + g + 1)
                    pool.tensor_tensor(w_l[:, g], w[:, g], w_h[:, g].bitcast(F32),
                                       ALU.subtract).then_inc(w_split, 1)
                    pool.tensor_tensor(w_sum[:, g, :], w[:, g, 0, :], w[:, g, 1, :], ALU.add).then_inc(w_summed, 1)
                if more:
                    scale_and_shift(0, i + 1)
                pool.wait_ge(at_high, i + 1)
                pool.tensor_tensor(at_l[:, :, :, :], adjT[:, :, :, :], at_h[:, :, :, :].bitcast(F32),
                                   ALU.subtract).then_inc(at_split, 1)

            steps(pool, step)

        @block.tensor
        def _(pe):
            def product(dst, terms, start=True, stop=True):
                for n, (lh, ll, rh, rl) in enumerate(terms):
                    first, last = start and n == 0, stop and n == len(terms) - 1
                    pe.matmul(dst, lh, rh, start=first, stop=False)
                    pe.matmul(dst, lh, rl, start=False, stop=False)
                    mm = pe.matmul(dst, ll, rh, start=False, stop=last)
                return mm

            def turn_h(dst, tile):
                for t in range(T):
                    mm = pe.transpose(dst[:, t * P:(t + 1) * P], h[:, t, tile * P:(tile + 1) * P], ident[:, :])
                return mm

            def turn_h0(i, dt):
                if dt == 0:
                    pe.wait_ge(h_done[0], T * (i + 1))
                if dt >= 2:
                    pe.wait_ge(hT_split, DT * i + dt - 1)
                turn_h(bank[TR_BANK + dt % 2], dt).then_inc(hT_psum, 1)

            pe.wait_ge(wqk_loaded, 32)
            for t in range(DT):
                for o in range(DT):
                    mm = pe.matmul(bank[t][:, :], xb[:, o, t * P:(t + 1) * P], x1[:, o, :],
                                   start=(o == 0), stop=(o == DT - 1))
                mm.then_inc(setup_psum, 1)
            pe.wait_ge(bq_spread, DT)
            for o in range(DT):
                mm = pe.matmul(bank[5][:, :], bq_b[:, o * P:(o + 1) * P],
                               xb[:, o, :], start=(o == 0), stop=(o == DT - 1))
            mm.then_inc(setup_psum, 1)
            pe.wait_ge(ident_done, 1)
            for dt in range(DT):
                turn_h0(0, dt)
            for t in range(DT):
                for o in range(DT):
                    pe.matmul(bank[4][:, t:t + 1], x1[:, o, t * P:(t + 1) * P], bk_c[:, o:o + 1],
                              start=(o == 0), stop=(o == DT - 1))
            for o in range(DT):
                mm = pe.matmul(bank[4][:, DT:DT + 1], bq_b[:, o * P:(o + 1) * P],
                               bk_c[:, o:o + 1], start=(o == 0), stop=(o == DT - 1))
            mm.then_inc(setup_psum, 1)
            pe.wait_ge(n_split, DT)
            pe.wait_ge(setup_small, 4)

            def step(i, layer0=True, layer1=True, more=True):
                j = i - 1
                first = isinstance(i, int) and i == 1

                def kp(dt):
                    pe.wait_ge(hT_split, DT * (i + 1))
                    if layer1:
                        pe.wait_ge(x1_done, T * j + dt + 1)
                    cols = slice(dt * P, (dt + 1) * P)
                    product(bank[L0_BANK + (dt + 2) % 4][:, :],
                            [(n_h[:, c, cols], n_l[:, c, cols], hT_h[:, c, :], hT_l[:, c, :]) for c in range(DT)]
                            ).then_inc(kp_psum, 1)

                def turn_adj(g):
                    pe.wait_ge(adj_scaled, i + 1)
                    if layer1 and g == 0:
                        pe.wait_ge(sum_inv_done, i)
                    for jt in range(NT):
                        for it in range(NT):
                            at = (jt * NT + it) * P
                            mm = pe.transpose(bank[TR_BANK + g][:, at:at + P],
                                              adj_in[:, NT * g + it, jt * P:(jt + 1) * P], ident[:, :])
                    mm.then_inc(at_psum, 1)

                def turn_g(dt):
                    if dt == 0:
                        pe.wait_ge(h_done[1], T * (j + 1))
                        if not layer0:
                            pe.wait_ge(sum_inv_done, i)
                    if dt < 2 and layer0:
                        pe.wait_ge(at_copied, G * i + dt + 1)
                    if dt >= 2:
                        pe.wait_ge(gT_split, DT * j + dt - 1)
                    turn_h(bank[TR_BANK + dt % 2], dt).then_inc(gT_psum, 1)

                def scores(g):
                    queries = slice(g * nodes, (g + 1) * nodes)
                    for kt in range(NT):
                        keys = slice(g * nodes + kt * P, g * nodes + (kt + 1) * P)
                        dst = bank[L0_BANK + g][:, kt * nodes:(kt + 1) * nodes]
                        terms = [(kz_h[:, c, keys], kz_l[:, c, keys], hT_h[:, c, queries], hT_l[:, c, queries])
                                 for c in range(DT)]
                        if g == 0 and kt == 0:
                            pe.wait_ge(kp_split, DT * i + DT - 1)
                            product(dst, terms[:-1], stop=False)
                            pe.wait_ge(kp_split, DT * (i + 1))
                            product(dst, terms[-1:], start=False)
                        else:
                            mm = product(dst, terms)
                    mm.then_inc(score_psum, 1)

                def project(dst, src_h, src_l, t, m_h, m_l, stop=True):
                    rows = slice(t * P, (t + 1) * P)
                    return product(dst, [(src_h[:, c, rows], src_l[:, c, rows], m_h[:, c, :], m_l[:, c, :])
                                         for c in range(DT)], stop=stop)

                def z(t):
                    if t == 0:
                        pe.wait_ge(gT_split, DT * (j + 1))
                        if first:
                            pe.wait_ge(weight_split, 3)
                    if t >= 2:
                        pe.wait_ge(z_split, T * j + t - 1)
                    elif not first:
                        pe.wait_ge(x2_done, T * j - 1 + t)
                    project(bank[L1_BANK + t % 2][:, :], gT_h, gT_l, t, wb_h, wb_l).then_inc(z_psum, 1)

                def v(t):
                    if t == 0 and not layer1:
                        pe.wait_ge(weight_split, 1)
                    if t >= 2:
                        pe.wait_ge(exp_done, NT * (G * i + t - 1))
                    project(bank[L0_BANK + (t + 2) % 4][:, :], hT_h, hT_l, t, wv_h, wv_l).then_inc(v_psum, 1)

                def l1_out(t):
                    g, it = divmod(t, NT)
                    if t < 2:
                        pe.wait_ge(z_split, T * j + t + 3)
                    else:
                        pe.wait_ge(x2_done, T * j + t - 1)
                    dst = bank[L1_BANK + t % 2][:, :]
                    project(dst, gT_h, gT_l, t, wa_h, wa_l, stop=False)
                    if t == 0:
                        pe.wait_ge(at_split, j + 1)
                    rows = slice(it * P, (it + 1) * P)
                    product(dst, [(at_h[:, g, c, rows], at_l[:, g, c, rows], kz_h[:, NT * g + c, :], kz_l[:, NT * g + c, :])
                                  for c in range(NT)], start=False).then_inc(l1_psum, 1)

                def sums():
                    pe.wait_ge(w_summed, G * (i + 1))
                    if more:
                        pe.wait_ge(hT_split, DT * (i + 1) + 3)
                    for t in range(T):
                        g, qt = divmod(t, NT)
                        mm = pe.matmul(bank[TR_BANK][:, t:t + 1], w_sum[:, g, qt * P:(qt + 1) * P], ones[:, :],
                                       start=True, stop=True)
                    mm.then_inc(sum_psum, 1)

                def av(t):
                    g, qt = divmod(t, NT)
                    if t == 0:
                        pe.wait_ge(v_split, T * (i + 1))
                        pe.wait_ge(w_split, G * (i + 1))
                    cols = slice(qt * P, (qt + 1) * P)
                    product(bank[L0_BANK + (t + 2) % 4][:, :],
                            [(w_h[:, g, c, cols], w_l[:, g, c, cols], v_h[:, NT * g + c, :], v_l[:, NT * g + c, :])
                             for c in range(NT)]).then_inc(av_psum, 1)

                if layer0:
                    kp(0)
                    turn_adj(0)
                    kp(1)
                    turn_adj(1)
                    kp(2)
                if layer1:
                    turn_g(0)
                if layer0:
                    kp(3)
                if layer1:
                    turn_g(1)
                    turn_g(2)
                if layer0:
                    scores(0)
                if layer1:
                    turn_g(3)
                if layer0:
                    scores(1)
                if layer1:
                    for t in range(T):
                        z(t)
                if layer0:
                    for t in range(T):
                        v(t)
                    if more and not layer1:
                        pe.wait_ge(at_copied, G)
                for t in range(T):
                    if layer1:
                        l1_out(t)
                    if more:
                        turn_h0(i + 1, t)
                if layer0:
                    sums()
                    for t in range(T):
                        av(t)

            steps(pe, step)

        @block.scalar
        def _(act):
            def high(dst, src, full, count, done):
                act.wait_ge(full, count)
                nc.scalar.activation(dst, src, ACT.Copy).then_inc(done, 1)

            def relu_norm(n, src, i, t):
                if t % NT == 0:
                    act.wait_ge(shift_done[n], G * i + t // NT + 1)
                nc.scalar.activation(h[:, t, :], src[:, t, :], ACT.Relu, bias=shift[n][:, t:t + 1],
                                     scale=rstd[n][:, t:t + 1]).then_inc(h_done[n], 1)

            def high_hT(i, dt):
                high(hT_h[:, dt, :], bank[TR_BANK + dt % 2][:, :], hT_psum, DT * i + dt + 1, hT_high)

            for t in range(T):
                relu_norm(0, x_in, 0, t)
            for t in range(DT):
                high(n_h[:, t, :], bank[t][:, :], setup_psum, t + 1, n_high)
            for dt in range(DT):
                high_hT(0, dt)

            def high_weight(n):
                act.wait_ge(weight_loaded[n], 16)
                nc.scalar.activation((wv_h, wa_h, wb_h)[n][:, :, :], x1[:, :, :], ACT.Copy).then_inc(weight_high, 1)

            high_weight(0)

            def step(i, layer0=True, layer1=True, more=True):
                j = i - 1

                def high_kp(dt):
                    if dt == 0 and not layer1:
                        act.wait_ge(setup_small, 4)
                    act.wait_ge(kp_psum, DT * i + dt + 1)
                    nc.scalar.activation(kz_h[:, dt, :], bank[L0_BANK + (dt + 2) % 4][:, :], ACT.Identity,
                                         bias=kp_bias[:, dt:dt + 1]).then_inc(kp_high, 1)

                def copy_adjT(g):
                    if layer1 and g == 0:
                        act.wait_ge(at_split, i)
                    act.wait_ge(at_psum, G * i + g + 1)
                    nc.scalar.activation(adjT[:, g, :, :], bank[TR_BANK + g][:, :].rearrange("p (t n) -> p t n", t=NT),
                                         ACT.Copy).then_inc(at_copied, 1)

                def high_gT(dt):
                    high(gT_h[:, dt, :], bank[TR_BANK + dt % 2][:, :], gT_psum, DT * j + dt + 1, gT_high)

                def exp(g):
                    if g == 0:
                        act.wait_ge(key_bias_done, T * (i + 1))
                    act.wait_ge(score_psum, G * i + g + 1)
                    for kt in range(NT):
                        nc.scalar.activation(w[:, g, kt, :], bank[L0_BANK + g][:, kt * nodes:(kt + 1) * nodes], ACT.Exp,
                                             bias=key_bias[:, NT * g + kt:NT * g + kt + 1]).then_inc(exp_done, 1)

                def high_z(t):
                    high(kz_h[:, t, :], bank[L1_BANK + t % 2][:, :], z_psum, T * j + t + 1, z_high)

                def high_w(g):
                    act.wait_ge(w_done, G * i + g + 1)
                    nc.scalar.activation(w_h[:, g], w[:, g], ACT.Copy).then_inc(w_high, 1)

                if layer1:
                    if layer0:
                        act.wait_ge(key_bias_done, T * (i + 1))
                    for t in range(T):
                        relu_norm(1, x1, j, t)
                if layer0:
                    high_kp(0)
                    copy_adjT(0)
                    high_kp(1)
                    copy_adjT(1)
                    high_kp(2)
                if layer1:
                    high_gT(0)
                if layer0:
                    high_kp(3)
                if layer1:
                    high_gT(1)
                    high_gT(2)
                if layer0:
                    exp(0)
                if layer1:
                    high_gT(3)
                if layer0:
                    exp(1)
                    high_w(0)
                    high_w(1)
                    if not layer1:
                        high_weight(1)
                if layer1:
                    high_z(0)
                    high_z(1)
                if more:
                    relu_norm(0, x_in, i + 1, 0)
                    relu_norm(0, x_in, i + 1, 1)
                if layer1:
                    high_z(2)
                if more:
                    relu_norm(0, x_in, i + 1, 2)
                    relu_norm(0, x_in, i + 1, 3)
                if layer1:
                    high_z(3)
                if layer0:
                    for t in range(T):
                        high(v_h[:, t, :], bank[L0_BANK + (t + 2) % 4][:, :], v_psum, T * i + t + 1, v_high)
                    if not layer1:
                        high_weight(2)
                if more:
                    for dt in range(DT):
                        high_hT(i + 1, dt)
                if layer0:
                    act.wait_ge(at_copied, G * (i + 1))
                    if layer1:
                        act.wait_ge(l1_psum, T * (j + 1))
                    nc.scalar.activation(at_h[:, :, :, :], adjT[:, :, :, :], ACT.Copy).then_inc(at_high, 1)

            steps(act, step)

        @block.vector
        def _(dve):
            def low(dst, src, high_part, high_done, count, done):
                dve.wait_ge(high_done, count)
                nc.vector.tensor_tensor(dst, src, high_part.bitcast(F32), ALU.subtract).then_inc(done, 1)

            def low_hT(i, dt):
                low(hT_l[:, dt, :], bank[TR_BANK + dt % 2][:, :], hT_h[:, dt, :], hT_high, DT * i + dt + 1, hT_split)

            def tile_stats(n, src, t):
                nc.vector.bn_stats(stats[n][:, t, :], src[:, t, :]).then_inc(stats_done[n], 1)

            def moments(n, i, g):
                tiles = slice(NT * g, NT * g + NT)
                dve.wait_ge(stats_done[n], T * i + NT * (g + 1))
                nc.vector.tensor_tensor(mean_sum[n][:, tiles], stats[n][:, tiles, 1], stats[n][:, tiles, 4],
                                        ALU.add).then_inc(moments_done[n], 1)
                for t in range(NT * g, NT * g + NT):
                    nc.vector.bn_aggr(mean_var[n][:, t, :], stats[n][:, t, :]).then_inc(aggr_done[n], 1)
                dve.wait_ge(aggr_done[n], T * i + NT * (g + 1))
                nc.vector.tensor_scalar(var_eps[n][:, tiles], mean_var[n][:, tiles, 1], LN_EPS, None,
                                        ALU.add).then_inc(moments_done[n], 1)

            def layer0_stats(i, g):
                dve.wait_ge(x_loaded, 16 * (i + 1))
                for t in range(NT * g, NT * (g + 1)):
                    tile_stats(0, x_in, t)
                moments(0, i, g)

            def scale_adj(i):
                dve.wait_ge(adj_loaded, 16 * (i + 1))
                nc.vector.tensor_reduce(deg[:, :], adj_in[:, :, :], AX_X, ALU.add).then_inc(deg_done, 1)
                dve.wait_ge(deg_done, 3 * i + 1)
                nc.vector.tensor_scalar(deg_max[:, :], deg[:, :], DEG_EPS, None, ALU.max).then_inc(deg_done, 1)
                dve.wait_ge(deg_done, 3 * i + 2)
                nc.vector.reciprocal(deg_inv[:, :], deg_max[:, :]).then_inc(deg_done, 1)
                dve.wait_ge(deg_done, 3 * i + 3)
                for t in range(T):
                    last = nc.vector.tensor_scalar(adj_in[:, t, :], adj_in[:, t, :], deg_inv[:, t:t + 1], None, ALU.mult)
                last.then_inc(adj_scaled, 1)

            def key_biases(i, ahead=True):
                dve.wait_ge(h_done[0], T * (i + 1))
                if ahead:
                    dve.wait_ge(exp_done, T * i)
                for t in range(T):
                    if ahead or t:
                        dve.wait_ge(key_bias_done, T * i + t)
                    nc.vector.tensor_tensor_reduce(scratch[:, :], h[:, t, :], u_b[:, :], 1.0, bqk[:, 0:1],
                                                   ALU.mult, ALU.add, key_bias[:, t:t + 1]).then_inc(key_bias_done, 1)

            dve.wait_ge(consts, 2)
            nc.vector.tensor_copy(ones[:, :], scratch[:, 0:1]).then_inc(setup_small, 1)
            dve.wait_ge(bias_loaded, 48)
            for o in range(DT):
                nc.vector.tensor_scalar(bq_b[:, o * P:(o + 1) * P], scratch[:, 0:P], bq_c[:, o:o + 1], None,
                                        ALU.mult).then_inc(bq_spread, 1)
            for g in range(G):
                layer0_stats(0, g)
            scale_adj(0)
            for t in range(DT):
                low(n_l[:, t, :], bank[t][:, :], n_h[:, t, :], n_high, t + 1, n_split)
            for dt in range(DT):
                low_hT(0, dt)
            dve.wait_ge(setup_psum, DT + 2)
            nc.vector.tensor_copy(u_b[:, :], bank[5][:, :]).then_inc(setup_small, 1)
            nc.vector.tensor_copy(kp_bias[:, :], bank[4][:, 0:DT]).then_inc(setup_small, 1)
            nc.vector.tensor_copy(bqk[:, :], bank[4][:, DT:DT + 1]).then_inc(setup_small, 1)
            dve.wait_ge(setup_small, 4)
            dve.wait_ge(bq_spread, DT)
            key_biases(0, ahead=False)

            def low_weight(n):
                hi, lo = ((wv_h, wv_l), (wa_h, wa_l), (wb_h, wb_l))[n]
                low(lo[:, :, :], x1[:, :, :], hi[:, :, :], weight_high, n + 1, weight_split)

            low_weight(0)

            def step(i, layer0=True, layer1=True, more=True):
                j = i - 1
                first = isinstance(i, int) and i == 1

                def low_kp(dt):
                    dve.wait_ge(kp_high, DT * i + dt + 1)
                    nc.vector.scalar_tensor_tensor(out=kz_l[:, dt, :], in0=bank[L0_BANK + (dt + 2) % 4][:, :],
                                                   scalar=kp_bias[:, dt:dt + 1], in1=kz_h[:, dt, :].bitcast(F32),
                                                   op0=ALU.add, op1=ALU.subtract).then_inc(kp_split, 1)

                def low_gT(dt):
                    low(gT_l[:, dt, :], bank[TR_BANK + dt % 2][:, :], gT_h[:, dt, :], gT_high, DT * j + dt + 1, gT_split)

                def weigh(g):
                    dve.wait_ge(at_copied, G * i + g + 1)
                    dve.wait_ge(exp_done, T * i + NT * (g + 1))
                    nc.vector.tensor_tensor(w[:, g], w[:, g], adjT[:, g], ALU.mult).then_inc(w_done, 1)

                def low_z(t):
                    low(kz_l[:, t, :], bank[L1_BANK + t % 2][:, :], kz_h[:, t, :], z_high, T * j + t + 1, z_split)

                def low_v(t):
                    low(v_l[:, t, :], bank[L0_BANK + (t + 2) % 4][:, :], v_h[:, t, :], v_high, T * i + t + 1, v_split)

                def layer1_result(t):
                    dve.wait_ge(l1_psum, T * j + t + 1)
                    if not (first and t < 2):
                        dve.wait_ge(out_stored[t % 2], 16 * (T // 2 * j + t // 2))
                    nc.vector.scalar_tensor_tensor(out=x2[:, t % 2, :], in0=bank[L1_BANK + t % 2][:, :], scalar=0.0,
                                                   in1=x1[:, t, :], op0=ALU.max, op1=ALU.add).then_inc(x2_done, 1)

                def layer0_result(t):
                    dve.wait_ge(xb_done, T * i + t + 1)
                    dve.wait_ge(av_psum, T * i + t + 1)
                    nc.vector.scalar_tensor_tensor(out=x1[:, t, :], in0=bank[L0_BANK + (t + 2) % 4][:, :],
                                                   scalar=sum_inv[:, t:t + 1], in1=xb[:, t, :],
                                                   op0=ALU.mult, op1=ALU.add).then_inc(x1_done, 1)
                    dve.wait_ge(x1_done, T * i + t + 1)
                    tile_stats(1, x1, t)

                if layer0:
                    low_kp(0)
                    low_kp(1)
                    low_kp(2)
                if layer1:
                    low_gT(0)
                if layer0:
                    low_kp(3)
                if layer1:
                    low_gT(1)
                    low_gT(2)
                if layer0:
                    weigh(0)
                if layer1:
                    low_gT(3)
                if layer0:
                    weigh(1)
                    if not layer1:
                        low_weight(1)
                if more:
                    layer0_stats(i + 1, 0)
                if layer1:
                    low_z(0)
                if more:
                    layer0_stats(i + 1, 1)
                if layer1:
                    low_z(1)
                if more:
                    scale_adj(i + 1)
                if layer1:
                    low_z(2)
                    low_z(3)
                if layer0:
                    low_v(0)
                    low_v(1)
                if more:
                    key_biases(i + 1)
                if layer0:
                    low_v(2)
                    low_v(3)
                    if not layer1:
                        low_weight(2)
                for t in range(T):
                    if layer1:
                        layer1_result(t)
                    if more:
                        low_hT(i + 1, t)
                if layer0:
                    dve.wait_ge(sum_psum, i + 1)
                    nc.vector.reciprocal(sum_inv[:, :], bank[TR_BANK][:, 0:T]).then_inc(sum_inv_done, 1)
                    dve.wait_ge(sum_inv_done, i + 1)
                    if layer1:
                        dve.wait_ge(x2_done, T * (j + 1))
                    for t in range(T):
                        layer0_result(t)
                        if t % NT == NT - 1:
                            moments(1, i, t // NT)

            steps(dve, step)


_OUT = (64, 256, 512)


def kernel(**inputs):
    import numpy as _np
    import concourse.bacc as _bacc
    from concourse.bass_utils import run_bass_kernel_spmd as _run

    arrays = {
        "x": inputs["x"], "adj": inputs["adj"],
        "wq": inputs["L0_gnn_Wq_w"], "bq": inputs["L0_gnn_Wq_b"],
        "wk": inputs["L0_gnn_Wk_w"], "bk": inputs["L0_gnn_Wk_b"],
        "wv_t": _np.transpose(inputs["L0_gnn_Wv_w"]), "bv": inputs["L0_gnn_Wv_b"],
        "w1_t": _np.transpose(inputs["L1_gnn_W"]),
    }
    arrays = {name: _np.ascontiguousarray(a) for name, a in arrays.items()}
    nc = _bacc.Bacc("TRN2", target_bir_lowering=False, num_devices=1)
    args = [nc.dram_tensor(name, a.shape, F32, kind="ExternalInput").ap() for name, a in arrays.items()]
    out = nc.dram_tensor("out", _OUT, F32, kind="ExternalOutput").ap()
    gnn_layers(nc, *args, out)
    r = _run(nc, [arrays], core_ids=[0])
    return r.results[0]["out"]
```

```python
from contextlib import ExitStack

import concourse.bass as bass
from concourse import mybir

F32 = mybir.dt.float32
F32R = mybir.dt.float32r
ALU = mybir.AluOpType
ACT = mybir.ActivationFunctionType
AX_X = mybir.AxisListType.X

P = 128
LN_EPS = 1e-5
DEG_EPS = 1e-6
L0_BANK, L1_BANK, TR_BANK = 0, 4, 6


def gnn_layers(nc, x, x_t, adj, adj_t, wq, bq, wk, bk, wv_t, bv, w1_t, out):
    graphs, nodes, dim = x.shape
    G = 2
    PAIRS = graphs // G
    NT = nodes // P
    T = G * NT
    DT = dim // P
    N = T * P
    assert graphs % G == 0 and PAIRS >= 4 and NT == 2 and T == 4 and DT == 4 and dim == 512

    x_d = x.rearrange("(i g) (t p) d -> i p (g t) d", g=G, p=P)
    adj_d = adj.rearrange("(i g) (t p) j -> i p (g t) j", g=G, p=P)
    adjT_d = adj_t.rearrange("(i g) (t p) n -> i p (g t) n", g=G, p=P)
    xT_d = x_t.rearrange("(i g) (c p) n -> i g p c n", g=G, p=P)
    out_d = out.rearrange("(i g) (t p) d -> i (g t) p d", g=G, p=P)

    norms_d = nc.dram_tensor("norms", (P, 2 * T), F32, kind="Internal").ap()

    with ExitStack() as ctx:
        def sb(name, shape, dt=F32):
            return ctx.enter_context(nc.sbuf_tensor(name, shape, dt))

        def sem(name):
            return ctx.enter_context(nc.semaphore(name))

        n_h, n_l = sb("n_h", [P, DT, dim], F32R), sb("n_l", [P, DT, dim], F32R)
        wv_h, wv_l = sb("wv_h", [P, DT, dim], F32R), sb("wv_l", [P, DT, dim], F32R)
        wa_h, wa_l = sb("wa_h", [P, DT, dim], F32R), sb("wa_l", [P, DT, dim], F32R)
        wb_h, wb_l = sb("wb_h", [P, DT, dim], F32R), sb("wb_l", [P, DT, dim], F32R)
        hT_h, hT_l = sb("hT_h", [P, DT, N], F32R), sb("hT_l", [P, DT, N], F32R)
        gT_h, gT_l = sb("gT_h", [P, DT, N], F32R), sb("gT_l", [P, DT, N], F32R)
        kz_h, kz_l = sb("kz_h", [P, 4, 512], F32R), sb("kz_l", [P, 4, 512], F32R)
        v_h, v_l = sb("v_h", [P, T, dim], F32R), sb("v_l", [P, T, dim], F32R)
        w_h, w_l = sb("w_h", [P, G, NT, nodes], F32R), sb("w_l", [P, G, NT, nodes], F32R)
        at_h, at_l = sb("at_h", [P, T, nodes], F32R), sb("at_l", [P, T, nodes], F32R)
        x_in = sb("x_in", [P, T, dim])
        xb = sb("xb", [P, T, dim])
        x1 = sb("x1", [P, T, dim])
        h = sb("h", [P, T, dim])
        xT = sb("xT", [P, DT, N])
        y = sb("y", [P, 2, dim])
        shared = sb("shared", [P, T * nodes])
        adj_in = shared[:, :].rearrange("p (t j) -> p t j", t=T)
        norms = shared[:, :].rearrange("q (p k) -> q k p", k=2 * T)
        adjT = sb("adjT", [P, T, nodes])
        w_sum = sb("w_sum", [P, G, nodes])
        w = sb("w", [P, G, NT, nodes])
        bq_b = w[:, :, :, :].rearrange("p g t n -> p (g t n)")
        shared_w = shared[:, :].rearrange("p (t o) -> p t o", o=dim)
        weight_pieces = [((wv_h, wv_l), slice(0, DT), wv_t, xT[:, :, :]),
                         ((wa_h, wa_l), slice(0, 2), w1_t[0:dim], y[:, :, :]),
                         ((wa_h, wa_l), slice(2, DT), w1_t[0:dim], shared_w),
                         ((wb_h, wb_l), slice(0, DT), w1_t[dim:2 * dim], x1[:, :, :])]
        PIECES = len(weight_pieces)
        ident = sb("ident", [P, P])
        ones = sb("ones", [P, 1])
        minus_half = sb("minus_half", [P, NT])
        bv_b = sb("bv_b", [P, dim])
        u_b = sb("u_b", [P, dim])
        bq_c, bk_c = sb("bq_c", [P, DT]), sb("bk_c", [P, DT])
        kp_bias = sb("kp_bias", [P, DT])
        bqk = sb("bqk", [P, 1])
        key_bias = sb("key_bias", [P, T])
        stats = [sb(f"stats{n}", [P, T, 6]) for n in range(2)]
        mean_var = [sb(f"mean_var{n}", [P, T, 2]) for n in range(2)]
        var_eps = [sb(f"var_eps{n}", [P, T]) for n in range(2)]
        mean_sum = [sb(f"mean_sum{n}", [P, T]) for n in range(2)]
        rs = [sb(f"rs{n}", [P, 2, T]) for n in range(2)]
        half_rstd = [sb(f"half_rstd{n}", [P, T]) for n in range(2)]
        deg, deg_max, deg_inv = sb("deg", [P, T]), sb("deg_max", [P, T]), sb("deg_inv", [P, T])
        sum_inv = sb("sum_inv", [P, T])

        bank = [ctx.enter_context(nc.psum_tensor(f"bank{b}", [P, 512], F32)) for b in range(8)]

        wqk_loaded = [sem(f"wqk_loaded{o}") for o in range(DT)]
        bias_loaded = sem("bias_loaded")
        weight_loaded = [sem(f"weight_loaded{n}") for n in range(PIECES)]
        consts, ident_zero, ident_done = sem("consts"), sem("ident_zero"), sem("ident_done")
        bq_spread, setup_psum = sem("bq_spread"), sem("setup_psum")
        n_high, n_split = sem("n_high"), sem("n_split")
        u_done, bias_columns_done = sem("u_done"), sem("bias_columns_done")
        weight_high, weight_split = sem("weight_high"), sem("weight_split")
        x_loaded, adj_loaded, adjT_loaded = sem("x_loaded"), sem("adj_loaded"), sem("adjT_loaded")
        xT_loaded, norms_stored, norms_loaded = sem("xT_loaded"), sem("norms_stored"), sem("norms_loaded")
        out_stored = [sem(f"out_stored{t}") for t in range(T)]
        xT_scaled, xT_shifted = sem("xT_scaled"), sem("xT_shifted")
        stats_done = [sem(f"stats_done{n}") for n in range(2)]
        aggr_done = [sem(f"aggr_done{n}") for n in range(2)]
        moments_done = [sem(f"moments_done{n}") for n in range(2)]
        rstd_done = [sem(f"rstd_done{n}") for n in range(2)]
        shift_done = [sem(f"shift_done{n}") for n in range(2)]
        h_done = [sem(f"h_done{n}") for n in range(2)]
        key_bias_done, xb_done = sem("key_bias_done"), sem("xb_done")
        deg_done = sem("deg_done")
        hT_psum, hT_high, hT_split = sem("hT_psum"), sem("hT_high"), sem("hT_split")
        gT_psum, gT_high, gT_split = sem("gT_psum"), sem("gT_high"), sem("gT_split")
        at_high, at_split = sem("at_high"), sem("at_split")
        kp_psum, kp_high, kp_split = sem("kp_psum"), sem("kp_high"), sem("kp_split")
        v_psum, v_high, v_split = sem("v_psum"), sem("v_high"), sem("v_split")
        z_psum, z_high, z_split = sem("z_psum"), sem("z_high"), sem("z_split")
        score_psum, exp_done = sem("score_psum"), sem("exp_done")
        w_done, w_high, w_split, w_summed = sem("w_done"), sem("w_high"), sem("w_split"), sem("w_summed")
        sum_psum, sum_inv_done = sem("sum_psum"), sem("sum_inv_done")
        av_psum, x1_done = sem("av_psum"), sem("x1_done")
        ha_psum, ha_copied = sem("ha_psum"), sem("ha_copied")
        az_psum, y_done, x2_done = sem("az_psum"), sem("y_done"), sem("x2_done")

        def steps(engine, step):
            step(0, layer1=False)
            step(1)
            with engine.Fori(2, PAIRS - 1) as i:
                step(i)
            step(PAIRS - 1, more=False)
            step(PAIRS, layer0=False, more=False)

        block = ctx.enter_context(nc.Block())

        @block.sync
        def _(sp):
            def load_x(i):
                sp.dma_start(x_in[:, :, :], x_d[i]).then_inc(x_loaded, 16)

            def load_adjT(i):
                sp.dma_start(adjT[:, :, :], adjT_d[i]).then_inc(adjT_loaded, 16)

            def load_xT(i):
                for g in range(G):
                    sp.dma_start(xT[:, :, g * nodes:(g + 1) * nodes], xT_d[i, g]).then_inc(xT_loaded, 16)

            for o in range(DT):
                rows = slice(o * P, (o + 1) * P)
                sp.dma_start(x1[:, o, :], wq[rows]).then_inc(wqk_loaded[o], 16)
                sp.dma_start(xb[:, o, :], wk[rows]).then_inc(wqk_loaded[o], 16)
            load_x(0)
            sp.dma_start(bq_c[:, :], bq.rearrange("(t p) -> p t", p=P),
                         allow_slow_non_contiguous=True).then_inc(bias_loaded, 16)
            sp.dma_start(bk_c[:, :], bk.rearrange("(t p) -> p t", p=P),
                         allow_slow_non_contiguous=True).then_inc(bias_loaded, 16)
            sp.dma_start(bv_b[:, :], bv.rearrange("(a d) -> a d", a=1).to_broadcast([P, dim])).then_inc(bias_loaded, 16)
            load_adjT(0)
            for n, (_, tiles, src, place) in enumerate(weight_pieces):
                if n == PIECES - 1:
                    sp.wait_ge(xb_done, T)
                    load_x(1)
                    sp.wait_ge(setup_psum, DT + 2)
                sp.dma_start(place, src.rearrange("(t p) o -> p t o", p=P)[:, tiles, :]).then_inc(weight_loaded[n], 16)
            sp.wait_ge(weight_split, 3)
            load_xT(1)

            def step(i, layer0=True, layer1=True, more=True):
                if layer1:
                    j = i - 1
                    sp.wait_ge(xT_shifted, DT * (i if layer0 else i - 1))
                    sp.dma_start(adj_in, adj_d[j]).then_inc(adj_loaded, 16)
                if layer1 and more:
                    sp.wait_ge(xb_done, T * (i + 1))
                    load_x(i + 1)
                    sp.wait_ge(hT_split, DT * (i + 1))
                    load_xT(i + 1)
                if more:
                    sp.wait_ge(shift_done[0], G * (i + 2))
                    sp.dma_start(norms_d, rs[0][:, :, :].rearrange("p k t -> p (k t)")).then_inc(norms_stored, 16)
                    sp.wait_ge(norms_stored, 16 * (i + 1))
                    sp.dma_start(shared[:, :], norms_d.rearrange("(a p) k -> a (p k)", a=1).to_broadcast([P, P * 2 * T])
                                 ).then_inc(norms_loaded, 16)
                if layer1:
                    for t in range(T):
                        sp.wait_ge(x2_done, T * j + t + 1)
                        sp.dma_start(out_d[j, t], (x1 if layer0 else x_in)[:, t, :]).then_inc(out_stored[t], 16)
                if more:
                    sp.wait_ge(at_split, i + 1)
                    load_adjT(i + 1)

            steps(sp, step)
            for t in range(T):
                sp.wait_ge(out_stored[t], 16 * PAIRS)

        @block.gpsimd
        def _(pool):
            pool.memset(minus_half[:, :], -0.5).then_inc(consts, 1)
            pool.memset(ones[:, :], 1.0).then_inc(consts, 1)
            pool.memset(w_sum[:, :, :], 1.0).then_inc(consts, 1)
            pool.memset(ident[:, :], 0.0).then_inc(ident_zero, 1)
            pool.wait_ge(ident_zero, 1)
            pool.affine_select(out=ident[:, :], in_=ident[:, :], compare_op=ALU.not_equal, fill=1.0,
                               base=0, pattern=[[-1, P]], channel_multiplier=1).then_inc(ident_done, 1)

            def scale_and_shift(n, i):
                for g in range(G):
                    tiles = slice(NT * g, NT * g + NT)
                    pool.wait_ge(moments_done[n], 2 * (G * i + g + 1))
                    pool.tensor_tensor(rs[n][:, 0, tiles], var_eps[n][:, tiles], minus_half[:, :],
                                       ALU.pow).then_inc(rstd_done[n], 1)
                    pool.wait_ge(rstd_done[n], 2 * (G * i + g) + 1)
                    pool.tensor_tensor(half_rstd[n][:, tiles], rs[n][:, 0, tiles], minus_half[:, :],
                                       ALU.mult).then_inc(rstd_done[n], 1)
                    pool.wait_ge(rstd_done[n], 2 * (G * i + g) + 2)
                    pool.tensor_tensor(rs[n][:, 1, tiles], mean_sum[n][:, tiles], half_rstd[n][:, tiles],
                                       ALU.mult).then_inc(shift_done[n], 1)

            def add_bv(i):
                pool.wait_ge(x_loaded, 16 * (i + 1))
                for t in range(T):
                    pool.tensor_tensor(xb[:, t, :], x_in[:, t, :], bv_b[:, :], ALU.add).then_inc(xb_done, 1)

            def xT_step(i, k):
                if k == 0:
                    pool.wait_ge(xT_loaded, 16 * G * i)
                    pool.wait_ge(norms_loaded, 16 * i)
                for c in range(DT):
                    if k:
                        pool.wait_ge(xT_scaled, DT * (i - 1) + c + 1)
                    tile = xT[:, c, :].rearrange("p (t n) -> p t n", t=T)
                    pool.tensor_tensor(tile, tile, norms[:, k * T:(k + 1) * T, :],
                                       (ALU.mult, ALU.add)[k]).then_inc((xT_scaled, xT_shifted)[k], 1)

            pool.wait_ge(consts, 3)
            scale_and_shift(0, 0)
            pool.wait_ge(bias_loaded, 48)
            pool.wait_ge(setup_psum, DT + 1)

            def step(i, layer0=True, layer1=True, more=True):
                if not layer0:
                    return
                if layer1:
                    scale_and_shift(1, i - 1)
                    pool.wait_ge(x1_done, T * i)
                add_bv(i)
                if not layer1:
                    scale_and_shift(0, i + 1)
                    xT_step(i + 1, 0)
                for g in range(G):
                    pool.wait_ge(w_high, G * i + g + 1)
                    pool.tensor_tensor(w_l[:, g], w[:, g], w_h[:, g].bitcast(F32),
                                       ALU.subtract).then_inc(w_split, 1)
                    pool.tensor_tensor(w_sum[:, g, :], w[:, g, 0, :], w[:, g, 1, :], ALU.add).then_inc(w_summed, 1)
                if layer1 and more:
                    scale_and_shift(0, i + 1)
                    xT_step(i + 1, 0)
                if more:
                    xT_step(i + 1, 1)
                else:
                    scale_and_shift(1, i)
                pool.wait_ge(at_high, i + 1)
                pool.tensor_tensor(at_l[:, :, :], adjT[:, :, :], at_h[:, :, :].bitcast(F32),
                                   ALU.subtract).then_inc(at_split, 1)

            steps(pool, step)

        @block.tensor
        def _(pe):
            def product(dst, terms, start=True, stop=True):
                for n, (lh, ll, rh, rl) in enumerate(terms):
                    first, last = start and n == 0, stop and n == len(terms) - 1
                    pe.matmul(dst, lh, rh, start=first, stop=False)
                    pe.matmul(dst, lh, rl, start=False, stop=False)
                    mm = pe.matmul(dst, ll, rh, start=False, stop=last)
                return mm

            def turn_h(dst, tile):
                for t in range(T):
                    mm = pe.transpose(dst[:, t * P:(t + 1) * P], h[:, t, tile * P:(tile + 1) * P], ident[:, :])
                return mm

            def turn_first(dt):
                if dt == 0:
                    pe.wait_ge(h_done[0], T)
                if dt >= 2:
                    pe.wait_ge(hT_split, dt - 1)
                turn_h(bank[TR_BANK + dt % 2], dt).then_inc(hT_psum, 1)

            for o in range(DT):
                pe.wait_ge(wqk_loaded[o], 32)
                for t in range(DT):
                    mm = pe.matmul(bank[t][:, :], xb[:, o, t * P:(t + 1) * P], x1[:, o, :],
                                   start=(o == 0), stop=(o == DT - 1))
                    if o == DT - 1:
                        mm.then_inc(setup_psum, 1)
            pe.wait_ge(bq_spread, DT)
            pe.wait_ge(ident_done, 1)
            for o in range(DT):
                mm = pe.matmul(bank[5][:, :], bq_b[:, o * P:(o + 1) * P], xb[:, o, :],
                               start=(o == 0), stop=(o == DT - 1))
                if o == DT - 1:
                    mm.then_inc(setup_psum, 1)
                turn_first(o)
            for t in range(DT):
                for o in range(DT):
                    pe.matmul(bank[4][:, t:t + 1], x1[:, o, t * P:(t + 1) * P], bk_c[:, o:o + 1],
                              start=(o == 0), stop=(o == DT - 1))
            for o in range(DT):
                mm = pe.matmul(bank[4][:, DT:DT + 1], bq_b[:, o * P:(o + 1) * P], bk_c[:, o:o + 1],
                               start=(o == 0), stop=(o == DT - 1))
            mm.then_inc(setup_psum, 1)
            pe.wait_ge(n_split, DT)

            def step(i, layer0=True, layer1=True, more=True):
                j = i - 1
                first = isinstance(i, int) and i == 1
                g_h, g_l = (gT_h, gT_l) if layer0 else (hT_h, hT_l)

                def kp(dt):
                    pe.wait_ge(hT_split, DT * (i + 1))
                    if layer1:
                        pe.wait_ge(x1_done, T * j + dt + 1)
                    cols = slice(dt * P, (dt + 1) * P)
                    product(bank[L0_BANK + (dt + 2) % 4][:, :],
                            [(n_h[:, c, cols], n_l[:, c, cols], hT_h[:, c, :], hT_l[:, c, :]) for c in range(DT)]
                            ).then_inc(kp_psum, 1)

                def turn_g(j, dt):
                    if dt == 0:
                        pe.wait_ge(h_done[1], T * (j + 1))
                        pe.wait_ge(sum_inv_done, j + 1)
                    if dt >= 2:
                        pe.wait_ge(gT_split, DT * j + dt - 1)
                    turn_h(bank[TR_BANK + dt % 2], dt).then_inc(gT_psum, 1)

                def scores(g):
                    queries = slice(g * nodes, (g + 1) * nodes)
                    for kt in range(NT):
                        keys = slice(g * nodes + kt * P, g * nodes + (kt + 1) * P)
                        dst = bank[L0_BANK + g][:, kt * nodes:(kt + 1) * nodes]
                        terms = [(kz_h[:, c, keys], kz_l[:, c, keys], hT_h[:, c, queries], hT_l[:, c, queries])
                                 for c in range(DT)]
                        if g == 0 and kt == 0:
                            pe.wait_ge(kp_split, DT * i + DT - 1)
                            product(dst, terms[:-1], stop=False)
                            pe.wait_ge(kp_split, DT * (i + 1))
                            product(dst, terms[-1:], start=False)
                        else:
                            mm = product(dst, terms)
                    mm.then_inc(score_psum, 1)

                def project(dst, src_h, src_l, t, m_h, m_l):
                    rows = slice(t * P, (t + 1) * P)
                    return product(dst, [(src_h[:, c, rows], src_l[:, c, rows], m_h[:, c, :], m_l[:, c, :])
                                         for c in range(DT)])

                def z(t):
                    if t == 0:
                        pe.wait_ge(gT_split, DT * (j + 1))
                        if first:
                            pe.wait_ge(weight_split, PIECES)
                    if t >= 2:
                        pe.wait_ge(z_split, T * j + t - 1)
                    elif not first:
                        pe.wait_ge((ha_copied, y_done)[t], T * j)
                    project(bank[L1_BANK + t % 2][:, :], g_h, g_l, t, wb_h, wb_l).then_inc(z_psum, 1)

                def v(t):
                    if t == 0 and not layer1:
                        pe.wait_ge(weight_split, 1)
                    if t >= 2:
                        pe.wait_ge(exp_done, NT * (G * i + t - 1))
                    project(bank[L0_BANK + (t + 2) % 4][:, :], hT_h, hT_l, t, wv_h, wv_l).then_inc(v_psum, 1)

                def layer1_products(t):
                    g, it = divmod(t, NT)
                    if t == 0:
                        pe.wait_ge(z_split, T * j + 3)
                    else:
                        pe.wait_ge(ha_copied, T * j + t)
                    project(bank[L1_BANK][:, :], g_h, g_l, t, wa_h, wa_l).then_inc(ha_psum, 1)
                    if t == 0:
                        pe.wait_ge(z_split, T * (j + 1))
                        pe.wait_ge(at_split, j + 1)
                    else:
                        pe.wait_ge(y_done, T * j + t)
                    rows = slice(it * P, (it + 1) * P)
                    tiles = range(NT * g, NT * (g + 1))
                    product(bank[L1_BANK + 1][:, :],
                            [(at_h[:, c, rows], at_l[:, c, rows], kz_h[:, c, :], kz_l[:, c, :]) for c in tiles]
                            ).then_inc(az_psum, 1)

                def sums():
                    pe.wait_ge(w_summed, G * (i + 1))
                    if not layer1:
                        pe.wait_ge(consts, 3)
                    pe.wait_ge(*((gT_split, DT * i) if layer1 else (hT_split, DT)))
                    for t in range(T):
                        g, qt = divmod(t, NT)
                        mm = pe.matmul(bank[TR_BANK][:, t:t + 1], w_sum[:, g, qt * P:(qt + 1) * P], ones[:, :],
                                       start=True, stop=True)
                    mm.then_inc(sum_psum, 1)

                def av(t):
                    g, qt = divmod(t, NT)
                    if t == 0:
                        pe.wait_ge(v_split, T * (i + 1))
                        pe.wait_ge(w_split, G * (i + 1))
                    cols = slice(qt * P, (qt + 1) * P)
                    product(bank[L0_BANK + (t + 2) % 4][:, :],
                            [(w_h[:, g, c, cols], w_l[:, g, c, cols], v_h[:, NT * g + c, :], v_l[:, NT * g + c, :])
                             for c in range(NT)]).then_inc(av_psum, 1)

                if layer0:
                    kp(0)
                    kp(1)
                    kp(2)
                    if layer1:
                        turn_g(j, 0)
                    kp(3)
                    if layer1:
                        turn_g(j, 1)
                        turn_g(j, 2)
                    scores(0)
                    if layer1:
                        turn_g(j, 3)
                    scores(1)
                if layer1:
                    for t in range(T):
                        z(t)
                if layer0:
                    for t in range(T):
                        v(t)
                if layer1 and more:
                    for t in range(T):
                        layer1_products(t)
                if layer0:
                    sums()
                    for t in range(T):
                        av(t)
                if not more:
                    layer1_products(0)
                    layer1_products(1)
                    if layer0:
                        turn_g(i, 0)
                    layer1_products(2)
                    if layer0:
                        turn_g(i, 1)
                    layer1_products(3)
                    if layer0:
                        turn_g(i, 2)
                        turn_g(i, 3)

            steps(pe, step)

        @block.scalar
        def _(act):
            def high(dst, src, full, count, done):
                act.wait_ge(full, count)
                nc.scalar.activation(dst, src, ACT.Copy).then_inc(done, 1)

            def relu_norm(n, src, i, t):
                if t % NT == 0:
                    act.wait_ge(shift_done[n], G * i + t // NT + 1)
                nc.scalar.activation(h[:, t, :], src[:, t, :], ACT.Relu, bias=rs[n][:, 1, t:t + 1],
                                     scale=rs[n][:, 0, t:t + 1]).then_inc(h_done[n], 1)

            def high_hT(i, dt):
                if dt == 0:
                    act.wait_ge(v_psum, T * i)
                act.wait_ge(xT_shifted, DT * (i - 1) + dt + 1)
                nc.scalar.activation(hT_h[:, dt, :], xT[:, dt, :], ACT.Relu).then_inc(hT_high, 1)

            for t in range(T):
                relu_norm(0, x_in, 0, t)
            for t in range(DT):
                high(n_h[:, t, :], bank[t][:, :], setup_psum, t + 1, n_high)
            for dt in range(DT):
                high(hT_h[:, dt, :], bank[TR_BANK + dt % 2][:, :], hT_psum, dt + 1, hT_high)

            def high_weight(n):
                (hi, _), tiles, _, place = weight_pieces[n]
                act.wait_ge(weight_loaded[n], 16)
                nc.scalar.activation(hi[:, tiles, :], place, ACT.Copy).then_inc(weight_high, 1)

            for n in range(PIECES - 1):
                high_weight(n)

            def step(i, layer0=True, layer1=True, more=True):
                j = i - 1
                first = isinstance(i, int) and i == 1

                def high_kp(dt):
                    if dt == 0 and not layer1:
                        act.wait_ge(bias_columns_done, 2)
                    act.wait_ge(kp_psum, DT * i + dt + 1)
                    nc.scalar.activation(kz_h[:, dt, :], bank[L0_BANK + (dt + 2) % 4][:, :], ACT.Identity,
                                         bias=kp_bias[:, dt:dt + 1]).then_inc(kp_high, 1)

                def high_gT(j, dt, dst=gT_h):
                    high(dst[:, dt, :], bank[TR_BANK + dt % 2][:, :], gT_psum, DT * j + dt + 1, gT_high)

                def copy_ha(t):
                    act.wait_ge(ha_psum, T * j + t + 1)
                    if not (first and t < 2):
                        act.wait_ge(x2_done, T * j + t - 1)
                    nc.scalar.activation(y[:, t % 2, :], bank[L1_BANK][:, :], ACT.Copy).then_inc(ha_copied, 1)

                def exp(g):
                    if g == 0:
                        act.wait_ge(key_bias_done, T * (i + 1))
                    act.wait_ge(score_psum, G * i + g + 1)
                    for kt in range(NT):
                        nc.scalar.activation(w[:, g, kt, :], bank[L0_BANK + g][:, kt * nodes:(kt + 1) * nodes], ACT.Exp,
                                             bias=key_bias[:, NT * g + kt:NT * g + kt + 1]).then_inc(exp_done, 1)

                def high_z(t):
                    high(kz_h[:, t, :], bank[L1_BANK + t % 2][:, :], z_psum, T * j + t + 1, z_high)

                def high_v(t):
                    high(v_h[:, t, :], bank[L0_BANK + (t + 2) % 4][:, :], v_psum, T * i + t + 1, v_high)

                def high_w(g):
                    act.wait_ge(w_done, G * i + g + 1)
                    nc.scalar.activation(w_h[:, g], w[:, g], ACT.Copy).then_inc(w_high, 1)

                if layer0:
                    if layer1:
                        act.wait_ge(key_bias_done, T * (i + 1))
                        for t in range(T):
                            relu_norm(1, x1, j, t)
                    high_kp(0)
                    high_kp(1)
                    high_kp(2)
                    if layer1:
                        high_gT(j, 0)
                    high_kp(3)
                    if layer1:
                        high_gT(j, 1)
                        high_gT(j, 2)
                    else:
                        high_weight(PIECES - 1)
                    exp(0)
                    if layer1:
                        high_gT(j, 3)
                    exp(1)
                    high_w(0)
                    high_w(1)
                if layer1:
                    high_z(0)
                    high_z(1)
                if not layer1:
                    high_v(0)
                if more:
                    relu_norm(0, x_in, i + 1, 0)
                    relu_norm(0, x_in, i + 1, 1)
                if layer1:
                    high_z(2)
                else:
                    high_v(1)
                if more:
                    relu_norm(0, x_in, i + 1, 2)
                    relu_norm(0, x_in, i + 1, 3)
                if layer1:
                    high_z(3)
                if layer0:
                    if layer1:
                        high_v(0)
                        high_v(1)
                    high_v(2)
                    high_v(3)
                if more:
                    for t in range(T):
                        if layer1:
                            copy_ha(t)
                        high_hT(i + 1, t)
                elif layer0:
                    copy_ha(0)
                    relu_norm(1, x_in, i, 0)
                    relu_norm(1, x_in, i, 1)
                    copy_ha(1)
                    relu_norm(1, x_in, i, 2)
                    relu_norm(1, x_in, i, 3)
                    high_gT(i, 0, hT_h)
                    copy_ha(2)
                    high_gT(i, 1, hT_h)
                    copy_ha(3)
                    high_gT(i, 2, hT_h)
                    high_gT(i, 3, hT_h)
                else:
                    for t in range(T):
                        copy_ha(t)
                if layer0:
                    act.wait_ge(adjT_loaded, 16 * (i + 1))
                    if layer1:
                        act.wait_ge(az_psum, T * (j + 1))
                    nc.scalar.activation(at_h[:, :, :], adjT[:, :, :], ACT.Copy).then_inc(at_high, 1)

            steps(act, step)

        @block.vector
        def _(dve):
            def low(dst, src, high_part, high_done, count, done):
                dve.wait_ge(high_done, count)
                nc.vector.tensor_tensor(dst, src, high_part.bitcast(F32), ALU.subtract).then_inc(done, 1)

            def low_hT(i, dt):
                dve.wait_ge(hT_high, DT * i + dt + 1)
                nc.vector.scalar_tensor_tensor(out=hT_l[:, dt, :], in0=xT[:, dt, :], scalar=0.0,
                                               in1=hT_h[:, dt, :].bitcast(F32), op0=ALU.max,
                                               op1=ALU.subtract).then_inc(hT_split, 1)

            def tile_stats(n, src, t):
                nc.vector.bn_stats(stats[n][:, t, :], src[:, t, :]).then_inc(stats_done[n], 1)

            def moments(n, i, g):
                tiles = slice(NT * g, NT * g + NT)
                dve.wait_ge(stats_done[n], T * i + NT * (g + 1))
                nc.vector.tensor_tensor(mean_sum[n][:, tiles], stats[n][:, tiles, 1], stats[n][:, tiles, 4],
                                        ALU.add).then_inc(moments_done[n], 1)
                for t in range(NT * g, NT * g + NT):
                    nc.vector.bn_aggr(mean_var[n][:, t, :], stats[n][:, t, :]).then_inc(aggr_done[n], 1)
                dve.wait_ge(aggr_done[n], T * i + NT * (g + 1))
                nc.vector.tensor_scalar(var_eps[n][:, tiles], mean_var[n][:, tiles, 1], LN_EPS, None,
                                        ALU.add).then_inc(moments_done[n], 1)

            def layer0_stats(i, g):
                dve.wait_ge(x_loaded, 16 * (i + 1))
                for t in range(NT * g, NT * (g + 1)):
                    tile_stats(0, x_in, t)
                moments(0, i, g)

            def degrees(i):
                dve.wait_ge(adj_loaded, 16 * (i + 1))
                nc.vector.tensor_reduce(deg[:, :], adj_in, AX_X, ALU.add).then_inc(deg_done, 1)
                dve.wait_ge(deg_done, 3 * i + 1)
                nc.vector.tensor_scalar(deg_max[:, :], deg[:, :], DEG_EPS, None, ALU.max).then_inc(deg_done, 1)
                dve.wait_ge(deg_done, 3 * i + 2)
                nc.vector.reciprocal(deg_inv[:, :], deg_max[:, :]).then_inc(deg_done, 1)

            def key_biases(i, g, ahead=True):
                dve.wait_ge(h_done[0], T * i + NT * (g + 1))
                if ahead and g == 0:
                    dve.wait_ge(exp_done, T * i)
                for t in range(NT * g, NT * (g + 1)):
                    nc.vector.tensor_tensor_reduce(h[:, t, :], h[:, t, :], u_b[:, :], 1.0, bqk[:, 0:1],
                                                   ALU.mult, ALU.add, key_bias[:, t:t + 1]).then_inc(key_bias_done, 1)

            dve.wait_ge(consts, 3)
            dve.wait_ge(bias_loaded, 48)
            for o in range(DT):
                nc.vector.tensor_scalar(bq_b[:, o * P:(o + 1) * P], w_sum[:, 0, 0:P], bq_c[:, o:o + 1], None,
                                        ALU.mult).then_inc(bq_spread, 1)
            for g in range(G):
                layer0_stats(0, g)
            for t in range(DT):
                low(n_l[:, t, :], bank[t][:, :], n_h[:, t, :], n_high, t + 1, n_split)
            for dt in range(DT):
                low(hT_l[:, dt, :], bank[TR_BANK + dt % 2][:, :], hT_h[:, dt, :], hT_high, dt + 1, hT_split)
            dve.wait_ge(setup_psum, DT + 1)
            nc.vector.tensor_copy(u_b[:, :], bank[5][:, :]).then_inc(u_done, 1)

            def low_weight(n):
                (hi, lo), tiles, _, place = weight_pieces[n]
                low(lo[:, tiles, :], place, hi[:, tiles, :], weight_high, n + 1, weight_split)

            for n in range(PIECES - 1):
                low_weight(n)
            dve.wait_ge(setup_psum, DT + 2)
            nc.vector.tensor_copy(kp_bias[:, :], bank[4][:, 0:DT]).then_inc(bias_columns_done, 1)
            nc.vector.tensor_copy(bqk[:, :], bank[4][:, DT:DT + 1]).then_inc(bias_columns_done, 1)
            for g in range(G):
                layer0_stats(1, g)
            dve.wait_ge(bias_columns_done, 2)
            dve.wait_ge(u_done, 1)

            def step(i, layer0=True, layer1=True, more=True):
                j = i - 1
                first = isinstance(i, int) and i == 1

                def low_kp(dt):
                    dve.wait_ge(kp_high, DT * i + dt + 1)
                    nc.vector.scalar_tensor_tensor(out=kz_l[:, dt, :], in0=bank[L0_BANK + (dt + 2) % 4][:, :],
                                                   scalar=kp_bias[:, dt:dt + 1], in1=kz_h[:, dt, :].bitcast(F32),
                                                   op0=ALU.add, op1=ALU.subtract).then_inc(kp_split, 1)

                def low_gT(j, dt, hi=gT_h, lo=gT_l):
                    low(lo[:, dt, :], bank[TR_BANK + dt % 2][:, :], hi[:, dt, :], gT_high, DT * j + dt + 1, gT_split)

                def weigh(g):
                    if g == 0:
                        dve.wait_ge(adjT_loaded, 16 * (i + 1))
                    dve.wait_ge(exp_done, T * i + NT * (g + 1))
                    nc.vector.tensor_tensor(w[:, g], w[:, g], adjT[:, NT * g:NT * (g + 1), :], ALU.mult).then_inc(w_done, 1)

                def low_z(t):
                    low(kz_l[:, t, :], bank[L1_BANK + t % 2][:, :], kz_h[:, t, :], z_high, T * j + t + 1, z_split)

                def low_v(t):
                    low(v_l[:, t, :], bank[L0_BANK + (t + 2) % 4][:, :], v_h[:, t, :], v_high, T * i + t + 1, v_split)

                def layer1_result(t):
                    dve.wait_ge(az_psum, T * j + t + 1)
                    dve.wait_ge(ha_copied, T * j + t + 1)
                    nc.vector.scalar_tensor_tensor(out=y[:, t % 2, :], in0=bank[L1_BANK + 1][:, :],
                                                   scalar=deg_inv[:, t:t + 1], in1=y[:, t % 2, :],
                                                   op0=ALU.mult, op1=ALU.add).then_inc(y_done, 1)
                    dve.wait_ge(y_done, T * j + t + 1)
                    place = (x1 if layer0 else x_in)[:, t, :]
                    nc.vector.scalar_tensor_tensor(out=place, in0=y[:, t % 2, :], scalar=0.0, in1=place,
                                                   op0=ALU.max, op1=ALU.add).then_inc(x2_done, 1)

                def layer0_result(t):
                    dst = x1 if more else x_in
                    dve.wait_ge(xb_done, T * i + t + 1)
                    dve.wait_ge(av_psum, T * i + t + 1)
                    if layer1 and more:
                        dve.wait_ge(out_stored[t], 16 * (j + 1))
                    nc.vector.scalar_tensor_tensor(out=dst[:, t, :], in0=bank[L0_BANK + (t + 2) % 4][:, :],
                                                   scalar=sum_inv[:, t:t + 1], in1=xb[:, t, :],
                                                   op0=ALU.mult, op1=ALU.add).then_inc(x1_done, 1)
                    dve.wait_ge(x1_done, T * i + t + 1)
                    tile_stats(1, dst, t)

                def layer0_results():
                    dve.wait_ge(sum_psum, i + 1)
                    nc.vector.reciprocal(sum_inv[:, :], bank[TR_BANK][:, 0:T]).then_inc(sum_inv_done, 1)
                    dve.wait_ge(sum_inv_done, i + 1)
                    for t in range(T):
                        layer0_result(t)
                        if t % NT == NT - 1:
                            moments(1, i, t // NT)

                if layer0:
                    low_kp(0)
                    low_kp(1)
                    if layer1:
                        degrees(j)
                    low_kp(2)
                    if layer1:
                        low_gT(j, 0)
                    low_kp(3)
                    if layer1:
                        low_gT(j, 1)
                        low_gT(j, 2)
                    else:
                        key_biases(0, 0, ahead=False)
                        key_biases(0, 1)
                        low_weight(PIECES - 1)
                    weigh(0)
                    if layer1:
                        low_gT(j, 3)
                    weigh(1)
                else:
                    degrees(j)
                if layer1 and more:
                    layer0_stats(i + 1, 0)
                if layer1:
                    low_z(0)
                if layer1 and more:
                    layer0_stats(i + 1, 1)
                if layer1:
                    low_z(1)
                    low_z(2)
                    low_z(3)
                if layer0:
                    low_v(0)
                    low_v(1)
                if more:
                    key_biases(i + 1, 0)
                if layer0:
                    low_v(2)
                if more:
                    key_biases(i + 1, 1)
                if layer0:
                    low_v(3)
                if layer1:
                    dve.wait_ge(deg_done, 3 * (j + 1))
                if more:
                    for t in range(T):
                        if layer1:
                            layer1_result(t)
                        low_hT(i + 1, t)
                    layer0_results()
                else:
                    if layer0:
                        layer0_results()
                    layer1_result(0)
                    layer1_result(1)
                    if layer0:
                        low_gT(i, 0, hT_h, hT_l)
                    layer1_result(2)
                    if layer0:
                        low_gT(i, 1, hT_h, hT_l)
                    layer1_result(3)
                    if layer0:
                        low_gT(i, 2, hT_h, hT_l)
                        low_gT(i, 3, hT_h, hT_l)

            steps(dve, step)


_OUT = (64, 256, 512)


def kernel(**inputs):
    import numpy as _np
    import concourse.bacc as _bacc
    from concourse.bass_utils import run_bass_kernel_spmd as _run

    arrays = {
        "x": inputs["x"], "x_t": _np.swapaxes(inputs["x"], 1, 2), "adj": inputs["adj"], "adj_t": _np.swapaxes(inputs["adj"], 1, 2),
        "wq": inputs["L0_gnn_Wq_w"], "bq": inputs["L0_gnn_Wq_b"],
        "wk": inputs["L0_gnn_Wk_w"], "bk": inputs["L0_gnn_Wk_b"],
        "wv_t": _np.transpose(inputs["L0_gnn_Wv_w"]), "bv": inputs["L0_gnn_Wv_b"],
        "w1_t": _np.transpose(inputs["L1_gnn_W"]),
    }
    arrays = {name: _np.ascontiguousarray(a) for name, a in arrays.items()}
    nc = _bacc.Bacc("TRN2", target_bir_lowering=False, num_devices=1)
    args = [nc.dram_tensor(name, a.shape, F32, kind="ExternalInput").ap() for name, a in arrays.items()]
    out = nc.dram_tensor("out", _OUT, F32, kind="ExternalOutput").ap()
    gnn_layers(nc, *args, out)
    r = _run(nc, [arrays], core_ids=[0])
    return r.results[0]["out"]
```

```python
from contextlib import ExitStack

import concourse.bass as bass
from concourse import mybir

F32 = mybir.dt.float32
F32R = mybir.dt.float32r
I32 = mybir.dt.int32
ALU = mybir.AluOpType
ACT = mybir.ActivationFunctionType
AX_X = mybir.AxisListType.X

P = 128
LN_EPS = 1e-5
DEG_EPS = 1e-6
L0_BANK, L1_BANK, TR_BANK = 0, 4, 6


def gnn_layers(nc, x, x_t, adj, adj_t, wq, bq, wk, bk, wv_t, bv, w1_t, out):
    graphs, nodes, dim = x.shape
    G = 2
    PAIRS = graphs // G
    NT = nodes // P
    T = G * NT
    DT = dim // P
    N = T * P
    assert graphs % G == 0 and PAIRS >= 4 and NT == 2 and T == 4 and DT == 4 and dim == 512

    x_d = x.rearrange("(i g) (t p) d -> i p (g t) d", g=G, p=P)
    adj_d = adj.rearrange("(i g) (t p) j -> i p (g t) j", g=G, p=P)
    adjT_d = adj_t.rearrange("(i g) (t p) n -> i p (g t) n", g=G, p=P)
    xT_d = x_t.rearrange("(i g) (c p) n -> i g p c n", g=G, p=P)
    out_d = out.rearrange("(i g) (t p) d -> i (g t) p d", g=G, p=P)

    norms_d = nc.dram_tensor("norms", (P, 2 * T), F32, kind="Internal").ap()

    with ExitStack() as ctx:
        def sb(name, shape, dt=F32):
            return ctx.enter_context(nc.sbuf_tensor(name, shape, dt))

        def sem(name):
            return ctx.enter_context(nc.semaphore(name))

        n_h, n_l = sb("n_h", [P, DT, dim], F32R), sb("n_l", [P, DT, dim], F32R)
        wv_h, wv_l = sb("wv_h", [P, DT, dim], F32R), sb("wv_l", [P, DT, dim], F32R)
        wa_h, wa_l = sb("wa_h", [P, DT, dim], F32R), sb("wa_l", [P, DT, dim], F32R)
        wb_h, wb_l = sb("wb_h", [P, DT, dim], F32R), sb("wb_l", [P, DT, dim], F32R)
        hT_h, hT_l = sb("hT_h", [P, DT, N], F32R), sb("hT_l", [P, DT, N], F32R)
        gT_h, gT_l = sb("gT_h", [P, DT, N], F32R), sb("gT_l", [P, DT, N], F32R)
        kz_h, kz_l = sb("kz_h", [P, 4, 512], F32R), sb("kz_l", [P, 4, 512], F32R)
        v_h, v_l = sb("v_h", [P, T, dim], F32R), sb("v_l", [P, T, dim], F32R)
        w_h, w_l = sb("w_h", [P, G, NT, nodes], F32R), sb("w_l", [P, G, NT, nodes], F32R)
        at_h, at_l = sb("at_h", [P, T, nodes], F32R), sb("at_l", [P, T, nodes], F32R)
        x_in = sb("x_in", [P, T, dim])
        xb = sb("xb", [P, T, dim])
        x1 = sb("x1", [P, T, dim])
        h = sb("h", [P, T, dim])
        xT = sb("xT", [P, DT, N])
        y = sb("y", [P, dim])
        shared = sb("shared", [P, T * nodes])
        adj_in = shared[:, :].rearrange("p (t j) -> p t j", t=T)
        norms = shared[:, :].rearrange("q (p k) -> q k p", k=2 * T)
        adjT = sb("adjT", [P, T, nodes])
        sum_h, sum_l = sb("sum_h", [P, G, nodes], F32R), sb("sum_l", [P, G, nodes], F32R)
        w = sb("w", [P, G, NT, nodes])
        wb_parts = w[:, :, :, :].rearrange("p g t n -> p g (t n)")
        shared_w = shared[:, :].rearrange("p (t o) -> p t o", o=dim)
        weight_pieces = [((wv_h, wv_l), slice(0, DT), wv_t, xT[:, :, :]),
                         ((wa_h, wa_l), slice(0, 2), w1_t[0:dim], shared_w),
                         ((wa_h, wa_l), slice(2, DT), w1_t[0:dim], wb_parts),
                         ((wb_h, wb_l), slice(0, DT), w1_t[dim:2 * dim], x1[:, :, :])]
        PIECES = len(weight_pieces)
        ident = sb("ident", [P, P])
        diagonal = sb("diagonal", [P, P], I32)
        ones = sb("ones", [P, 2], F32R)
        minus_half = sb("minus_half", [P, NT])
        bv_b = sb("bv_b", [P, dim])
        u_b = sb("u_b", [P, dim])
        bq_c, bk_c = sb("bq_c", [P, DT]), sb("bk_c", [P, DT])
        kp_bias = sb("kp_bias", [P, DT])
        bqk = sb("bqk", [P, 1])
        key_bias = sb("key_bias", [P, T])
        stats = [sb(f"stats{n}", [P, T, 6]) for n in range(2)]
        mean_var = [sb(f"mean_var{n}", [P, T, 2]) for n in range(2)]
        var_eps = [sb(f"var_eps{n}", [P, T]) for n in range(2)]
        mean_sum = [sb(f"mean_sum{n}", [P, T]) for n in range(2)]
        rs = [sb(f"rs{n}", [P, 2, T]) for n in range(2)]
        half_rstd = [sb(f"half_rstd{n}", [P, T]) for n in range(2)]
        deg, deg_inv = sb("deg", [P, T]), sb("deg_inv", [P, T])
        sums, sum_inv = sb("sums", [P, T]), sb("sum_inv", [P, T])

        bank = [ctx.enter_context(nc.psum_tensor(f"bank{b}", [P, 512], F32)) for b in range(8)]

        wqk_loaded = [sem(f"wqk_loaded{o}") for o in range(DT)]
        bias_loaded, bv_loaded = sem("bias_loaded"), sem("bv_loaded")
        weight_loaded = [sem(f"weight_loaded{n}") for n in range(PIECES)]
        consts, ident_zero, ident_done = sem("consts"), sem("ident_zero"), sem("ident_done")
        diagonal_done = sem("diagonal_done")
        parts_done, setup_psum = sem("parts_done"), sem("setup_psum")
        n_high, n_split = sem("n_high"), sem("n_split")
        u_done, bias_columns_done = sem("u_done"), sem("bias_columns_done")
        weight_high, weight_split = sem("weight_high"), sem("weight_split")
        x_loaded, adj_loaded, adjT_loaded = sem("x_loaded"), sem("adj_loaded"), sem("adjT_loaded")
        xT_loaded, norms_stored, norms_loaded = sem("xT_loaded"), sem("norms_stored"), sem("norms_loaded")
        out_stored = [sem(f"out_stored{t}") for t in range(T)]
        xT_scaled, xT_shifted = sem("xT_scaled"), sem("xT_shifted")
        stats_done = [sem(f"stats_done{n}") for n in range(2)]
        aggr_done = [sem(f"aggr_done{n}") for n in range(2)]
        moments_done = [sem(f"moments_done{n}") for n in range(2)]
        rstd_done = [sem(f"rstd_done{n}") for n in range(2)]
        shift_done = [sem(f"shift_done{n}") for n in range(2)]
        h_done = [sem(f"h_done{n}") for n in range(2)]
        key_bias_done, xb_done = sem("key_bias_done"), sem("xb_done")
        deg_done = sem("deg_done")
        hT_psum, hT_high, hT_split = sem("hT_psum"), sem("hT_high"), sem("hT_split")
        gT_psum, gT_high, gT_split = sem("gT_psum"), sem("gT_high"), sem("gT_split")
        at_high, at_split = sem("at_high"), sem("at_split")
        kp_psum, kp_high, kp_split = sem("kp_psum"), sem("kp_high"), sem("kp_split")
        v_psum, v_high, v_split = sem("v_psum"), sem("v_high"), sem("v_split")
        z_psum, z_high, z_split = sem("z_psum"), sem("z_high"), sem("z_split")
        score_psum, exp_done = sem("score_psum"), sem("exp_done")
        w_done, w_high, w_split, w_summed = sem("w_done"), sem("w_high"), sem("w_split"), sem("w_summed")
        sum_taken = sem("sum_taken")
        sum_high, sum_split = sem("sum_high"), sem("sum_split")
        sum_psum, sum_inv_done = sem("sum_psum"), sem("sum_inv_done")
        av_psum, x1_done = sem("av_psum"), sem("x1_done")
        ha_psum, ha_copied = sem("ha_psum"), sem("ha_copied")
        az_psum, y_done, x2_done = sem("az_psum"), sem("y_done"), sem("x2_done")

        def steps(engine, step):
            step(0, layer1=False)
            step(1)
            with engine.Fori(2, PAIRS - 1) as i:
                step(i)
            step(PAIRS - 1, more=False)
            step(PAIRS, layer0=False, more=False)

        def split_w(engine, i, g):
            engine.wait_ge(w_high, G * i + g + 1)
            engine.tensor_tensor(w_l[:, g], w[:, g], w_h[:, g].bitcast(F32), ALU.subtract).then_inc(w_split, 1)
            engine.wait_ge(w_split, G * i + g + 1)
            engine.tensor_tensor(w[:, g, 0, :], w[:, g, 0, :], w[:, g, 1, :], ALU.add).then_inc(w_summed, 1)

        block = ctx.enter_context(nc.Block())

        @block.sync
        def _(sp):
            def load_x(i):
                sp.dma_start(x_in[:, :, :], x_d[i]).then_inc(x_loaded, 16)

            def load_adjT(i):
                sp.dma_start(adjT[:, :, :], adjT_d[i]).then_inc(adjT_loaded, 16)

            def load_xT(i):
                for g in range(G):
                    sp.dma_start(xT[:, :, g * nodes:(g + 1) * nodes], xT_d[i, g]).then_inc(xT_loaded, 16)

            for o in range(DT):
                rows = slice(o * P, (o + 1) * P)
                sp.dma_start(x1[:, o, :], wq[rows]).then_inc(wqk_loaded[o], 16)
                sp.dma_start(xb[:, o, :], wk[rows]).then_inc(wqk_loaded[o], 16)
            sp.dma_start(bq_c[:, :], bq.rearrange("(t p) -> p t", p=P),
                         allow_slow_non_contiguous=True).then_inc(bias_loaded, 16)
            sp.dma_start(bk_c[:, :], bk.rearrange("(t p) -> p t", p=P),
                         allow_slow_non_contiguous=True).then_inc(bias_loaded, 16)
            load_x(0)
            sp.dma_start(bv_b[:, :], bv.rearrange("(a d) -> a d", a=1).to_broadcast([P, dim])).then_inc(bv_loaded, 16)
            load_adjT(0)

            def load_weight(n):
                _, tiles, src, place = weight_pieces[n]
                sp.dma_start(place, src.rearrange("(t p) o -> p t o", p=P)[:, tiles, :]).then_inc(weight_loaded[n], 16)

            load_weight(0)
            load_weight(1)
            sp.wait_ge(xb_done, T)
            load_x(1)
            sp.wait_ge(weight_split, 2)
            load_xT(1)
            sp.wait_ge(setup_psum, DT + 2)
            load_weight(2)

            def step(i, layer0=True, layer1=True, more=True):
                if layer1:
                    j = i - 1
                    sp.wait_ge(xT_shifted, DT * (i if layer0 else i - 1))
                    sp.dma_start(adj_in, adj_d[j]).then_inc(adj_loaded, 16)
                if layer1 and more:
                    sp.wait_ge(xb_done, T * (i + 1))
                    load_x(i + 1)
                    sp.wait_ge(hT_split, DT * (i + 1))
                    load_xT(i + 1)
                if more:
                    sp.wait_ge(shift_done[0], G * (i + 2))
                    sp.dma_start(norms_d, rs[0][:, :, :].rearrange("p k t -> p (k t)")).then_inc(norms_stored, 16)
                    sp.wait_ge(norms_stored, 16 * (i + 1))
                    sp.dma_start(shared[:, :], norms_d.rearrange("(a p) k -> a (p k)", a=1).to_broadcast([P, P * 2 * T])
                                 ).then_inc(norms_loaded, 16)
                if not layer1:
                    load_weight(3)
                if layer1:
                    for t in range(T):
                        sp.wait_ge(x2_done, T * j + t + 1)
                        sp.dma_start(out_d[j, t], (x1 if layer0 else x_in)[:, t, :]).then_inc(out_stored[t], 16)
                if more:
                    sp.wait_ge(at_split, i + 1)
                    load_adjT(i + 1)

            steps(sp, step)
            for t in range(T):
                sp.wait_ge(out_stored[t], 16 * PAIRS)

        @block.gpsimd
        def _(pool):
            pool.memset(minus_half[:, :], -0.5).then_inc(consts, 1)
            pool.memset(y[:, :], 1.0).then_inc(consts, 1)
            pool.memset(ident[:, :], 0.0).then_inc(ident_zero, 1)
            pool.wait_ge(ident_zero, 1)
            pool.affine_select(out=ident[:, :], in_=ident[:, :], compare_op=ALU.not_equal, fill=1.0,
                               base=0, pattern=[[-1, P]], channel_multiplier=1).then_inc(ident_done, 1)
            pool.wait_ge(ident_done, 1)
            pool.tensor_scalar(diagonal[:, :], ident[:, :], -1.0, None, ALU.mult).then_inc(diagonal_done, 1)

            def scale_and_shift(n, i):
                for g in range(G):
                    tiles = slice(NT * g, NT * g + NT)
                    pool.wait_ge(moments_done[n], 2 * (G * i + g + 1))
                    pool.tensor_tensor(rs[n][:, 0, tiles], var_eps[n][:, tiles], minus_half[:, :],
                                       ALU.pow).then_inc(rstd_done[n], 1)
                    pool.wait_ge(rstd_done[n], 2 * (G * i + g) + 1)
                    pool.tensor_tensor(half_rstd[n][:, tiles], rs[n][:, 0, tiles], minus_half[:, :],
                                       ALU.mult).then_inc(rstd_done[n], 1)
                    pool.wait_ge(rstd_done[n], 2 * (G * i + g) + 2)
                    pool.tensor_tensor(rs[n][:, 1, tiles], mean_sum[n][:, tiles], half_rstd[n][:, tiles],
                                       ALU.mult).then_inc(shift_done[n], 1)

            def add_bv(i):
                pool.wait_ge(x_loaded, 16 * (i + 1))
                for t in range(T):
                    pool.tensor_tensor(xb[:, t, :], x_in[:, t, :], bv_b[:, :], ALU.add).then_inc(xb_done, 1)

            def xT_step(i, k):
                if k == 0:
                    pool.wait_ge(xT_loaded, 16 * G * i)
                    pool.wait_ge(norms_loaded, 16 * i)
                for c in range(DT):
                    if k:
                        pool.wait_ge(xT_scaled, DT * (i - 1) + c + 1)
                    tile = xT[:, c, :].rearrange("p (t n) -> p t n", t=T)
                    pool.tensor_tensor(tile, tile, norms[:, k * T:(k + 1) * T, :],
                                       (ALU.mult, ALU.add)[k]).then_inc((xT_scaled, xT_shifted)[k], 1)

            pool.wait_ge(consts, 2)
            pool.tensor_copy(ones[:, :], y[:, 0:2]).then_inc(consts, 1)
            scale_and_shift(0, 0)
            pool.wait_ge(bv_loaded, 16)
            pool.wait_ge(setup_psum, DT + 1)

            def step(i, layer0=True, layer1=True, more=True):
                if not layer0:
                    return
                if layer1:
                    scale_and_shift(1, i - 1)
                    pool.wait_ge(x1_done, T * i)
                add_bv(i)
                if not layer1:
                    scale_and_shift(0, i + 1)
                    xT_step(i + 1, 0)
                if layer1:
                    for g in range(G):
                        split_w(pool, i, g)
                if layer1 and more:
                    scale_and_shift(0, i + 1)
                    xT_step(i + 1, 0)
                pool.wait_ge(sum_high, i + 1)
                pool.tensor_tensor(sum_l[:, :, :], w[:, :, 0, :], sum_h[:, :, :].bitcast(F32),
                                   ALU.subtract).then_inc(sum_split, 1)
                if more:
                    xT_step(i + 1, 1)
                else:
                    scale_and_shift(1, i)
                pool.wait_ge(at_high, i + 1)
                pool.tensor_tensor(at_l[:, :, :], adjT[:, :, :], at_h[:, :, :].bitcast(F32),
                                   ALU.subtract).then_inc(at_split, 1)

            steps(pool, step)

        @block.tensor
        def _(pe):
            def product(dst, terms, start=True, stop=True):
                for n, (lh, ll, rh, rl) in enumerate(terms):
                    first, last = start and n == 0, stop and n == len(terms) - 1
                    pe.matmul(dst, lh, rh, start=first, stop=False)
                    pe.matmul(dst, lh, rl, start=False, stop=False)
                    mm = pe.matmul(dst, ll, rh, start=False, stop=last)
                return mm

            def turn_h(dst, tile):
                for t in range(T):
                    mm = pe.transpose(dst[:, t * P:(t + 1) * P], h[:, t, tile * P:(tile + 1) * P], ident[:, :])
                return mm

            def turn_first(dt):
                if dt == 0:
                    pe.wait_ge(h_done[0], T)
                if dt >= 2:
                    pe.wait_ge(hT_split, dt - 1)
                turn_h(bank[TR_BANK + dt % 2], dt).then_inc(hT_psum, 1)

            for o in range(DT):
                pe.wait_ge(wqk_loaded[o], 32)
                for t in range(DT):
                    mm = pe.matmul(bank[t][:, :], xb[:, o, t * P:(t + 1) * P], x1[:, o, :],
                                   start=(o == 0), stop=(o == DT - 1))
                    if o == DT - 1:
                        mm.then_inc(setup_psum, 1)
            pe.wait_ge(ident_done, 1)
            turn_first(0)
            turn_first(1)
            pe.wait_ge(consts, 2)
            pe.wait_ge(parts_done, 2 * DT + 1)
            ones_f = y[:, 0:P]
            pe.matmul(bank[5][:, :], ones_f, wb_parts[:, 0, :], start=True, stop=True).then_inc(setup_psum, 1)
            turn_first(2)
            turn_first(3)
            for t in range(DT):
                pe.matmul(bank[4][:, t:t + 1], wb_parts[:, 1, t * P:(t + 1) * P], ones_f[:, 0:1], start=True, stop=True)
            pe.matmul(bank[4][:, DT:DT + 1], ones_f, sums[:, 0:1], start=True, stop=True).then_inc(setup_psum, 1)
            pe.wait_ge(n_split, DT)

            def step(i, layer0=True, layer1=True, more=True):
                j = i - 1
                first = isinstance(i, int) and i == 1
                g_h, g_l = (gT_h, gT_l) if layer0 else (hT_h, hT_l)

                def kp(dt):
                    pe.wait_ge(hT_split, DT * (i + 1))
                    if layer1:
                        pe.wait_ge(x1_done, T * j + dt + 1)
                    cols = slice(dt * P, (dt + 1) * P)
                    product(bank[L0_BANK + (dt + 2) % 4][:, :],
                            [(n_h[:, c, cols], n_l[:, c, cols], hT_h[:, c, :], hT_l[:, c, :]) for c in range(DT)]
                            ).then_inc(kp_psum, 1)

                def turn_g(j, dt):
                    if dt == 0:
                        pe.wait_ge(h_done[1], T * (j + 1))
                        pe.wait_ge(sum_inv_done, j + 1)
                    if dt >= 2:
                        pe.wait_ge(gT_split, DT * j + dt - 1)
                    turn_h(bank[TR_BANK + dt % 2], dt).then_inc(gT_psum, 1)

                def scores(g):
                    queries = slice(g * nodes, (g + 1) * nodes)
                    for kt in range(NT):
                        keys = slice(g * nodes + kt * P, g * nodes + (kt + 1) * P)
                        dst = bank[L0_BANK + g][:, kt * nodes:(kt + 1) * nodes]
                        terms = [(kz_h[:, c, keys], kz_l[:, c, keys], hT_h[:, c, queries], hT_l[:, c, queries])
                                 for c in range(DT)]
                        if g == 0 and kt == 0:
                            pe.wait_ge(kp_split, DT * i + DT - 1)
                            product(dst, terms[:-1], stop=False)
                            pe.wait_ge(kp_split, DT * (i + 1))
                            product(dst, terms[-1:], start=False)
                        else:
                            mm = product(dst, terms)
                    mm.then_inc(score_psum, 1)

                def project(dst, src_h, src_l, t, m_h, m_l):
                    rows = slice(t * P, (t + 1) * P)
                    return product(dst, [(src_h[:, c, rows], src_l[:, c, rows], m_h[:, c, :], m_l[:, c, :])
                                         for c in range(DT)])

                def z(t):
                    if t == 0:
                        pe.wait_ge(gT_split, DT * (j + 1))
                        if first:
                            pe.wait_ge(weight_split, PIECES)
                    if t >= 2:
                        pe.wait_ge(z_split, T * j + t - 1)
                    elif not first:
                        pe.wait_ge((ha_copied, y_done)[t], T * j)
                    project(bank[L1_BANK + t % 2][:, :], g_h, g_l, t, wb_h, wb_l).then_inc(z_psum, 1)

                def v(t):
                    if t == 0 and not layer1:
                        pe.wait_ge(weight_split, 1)
                    if t >= 2:
                        pe.wait_ge(exp_done, NT * (G * i + t - 1))
                    project(bank[L0_BANK + (t + 2) % 4][:, :], hT_h, hT_l, t, wv_h, wv_l).then_inc(v_psum, 1)

                def layer1_products(t):
                    g, it = divmod(t, NT)
                    if t == 0:
                        pe.wait_ge(z_split, T * j + 3)
                    else:
                        pe.wait_ge(ha_copied, T * j + t)
                    project(bank[L1_BANK][:, :], g_h, g_l, t, wa_h, wa_l).then_inc(ha_psum, 1)
                    if t == 0:
                        pe.wait_ge(z_split, T * (j + 1))
                        pe.wait_ge(at_split, j + 1)
                    else:
                        pe.wait_ge(y_done, T * j + t)
                    rows = slice(it * P, (it + 1) * P)
                    tiles = range(NT * g, NT * (g + 1))
                    product(bank[L1_BANK + 1][:, :],
                            [(at_h[:, c, rows], at_l[:, c, rows], kz_h[:, c, :], kz_l[:, c, :]) for c in tiles]
                            ).then_inc(az_psum, 1)

                def sums():
                    pe.wait_ge(sum_split, i + 1)
                    if not layer1:
                        pe.wait_ge(consts, 3)
                    pe.wait_ge(*((gT_split, DT * i) if layer1 else (hT_split, DT)))
                    every, all_ones = bank[TR_BANK][:, :], ones[:, 0:1].to_broadcast([P, P])
                    pe.matmul(every, all_ones, sum_h[:, :, :].rearrange("p g n -> p (g n)"), start=True, stop=False)
                    mm = pe.matmul(every, all_ones, sum_l[:, :, :].rearrange("p g n -> p (g n)"), start=False, stop=True)
                    mm.then_inc(sum_psum, 1)

                def av(t):
                    g, qt = divmod(t, NT)
                    if qt == 0:
                        pe.wait_ge(v_split, T * i + NT * (g + 1))
                        pe.wait_ge(w_split, G * i + g + 1)
                    cols = slice(qt * P, (qt + 1) * P)
                    product(bank[L0_BANK + (t + 2) % 4][:, :],
                            [(w_h[:, g, c, cols], w_l[:, g, c, cols], v_h[:, NT * g + c, :], v_l[:, NT * g + c, :])
                             for c in range(NT)]).then_inc(av_psum, 1)

                if layer0:
                    kp(0)
                    kp(1)
                    kp(2)
                    kp(3)
                    if layer1:
                        turn_g(j, 0)
                        turn_g(j, 1)
                    scores(0)
                    if layer1:
                        turn_g(j, 2)
                        turn_g(j, 3)
                    scores(1)
                if layer1:
                    for t in range(T):
                        z(t)
                if layer0:
                    for t in range(T):
                        v(t)
                if layer1 and more:
                    for t in range(T):
                        layer1_products(t)
                if layer0:
                    if layer1:
                        sums()
                    for t in range(T):
                        av(t)
                        if not layer1 and t == 1:
                            sums()
                if not more:
                    layer1_products(0)
                    layer1_products(1)
                    if layer0:
                        turn_g(i, 0)
                        turn_g(i, 1)
                    layer1_products(2)
                    if layer0:
                        turn_g(i, 2)
                        turn_g(i, 3)
                    layer1_products(3)

            steps(pe, step)

        @block.scalar
        def _(act):
            def high(dst, src, full, count, done):
                act.wait_ge(full, count)
                nc.scalar.activation(dst, src, ACT.Copy).then_inc(done, 1)

            def relu_norm(n, src, i, t):
                if t % NT == 0:
                    act.wait_ge(shift_done[n], G * i + t // NT + 1)
                nc.scalar.activation(h[:, t, :], src[:, t, :], ACT.Relu, bias=rs[n][:, 1, t:t + 1],
                                     scale=rs[n][:, 0, t:t + 1]).then_inc(h_done[n], 1)

            def high_hT(i, dt):
                if dt == 0:
                    act.wait_ge(v_psum, T * i)
                act.wait_ge(xT_shifted, DT * (i - 1) + dt + 1)
                nc.scalar.activation(hT_h[:, dt, :], xT[:, dt, :], ACT.Relu).then_inc(hT_high, 1)

            for t in range(T):
                relu_norm(0, x_in, 0, t)
            for t in range(DT):
                high(n_h[:, t, :], bank[t][:, :], setup_psum, t + 1, n_high)
            for dt in range(DT):
                high(hT_h[:, dt, :], bank[TR_BANK + dt % 2][:, :], hT_psum, dt + 1, hT_high)

            def high_weight(n):
                (hi, _), tiles, _, place = weight_pieces[n]
                act.wait_ge(weight_loaded[n], 16)
                nc.scalar.activation(hi[:, tiles, :], place, ACT.Copy).then_inc(weight_high, 1)

            high_weight(0)
            high_weight(1)

            def step(i, layer0=True, layer1=True, more=True):
                j = i - 1
                first = isinstance(i, int) and i == 1

                def high_kp(dt):
                    if dt == 0 and not layer1:
                        act.wait_ge(bias_columns_done, 2)
                    act.wait_ge(kp_psum, DT * i + dt + 1)
                    nc.scalar.activation(kz_h[:, dt, :], bank[L0_BANK + (dt + 2) % 4][:, :], ACT.Identity,
                                         bias=kp_bias[:, dt:dt + 1]).then_inc(kp_high, 1)

                def high_gT(j, dt, dst=gT_h):
                    high(dst[:, dt, :], bank[TR_BANK + dt % 2][:, :], gT_psum, DT * j + dt + 1, gT_high)

                def copy_ha(t):
                    act.wait_ge(ha_psum, T * j + t + 1)
                    if not (first and t == 0):
                        act.wait_ge(x2_done, T * j + t)
                    nc.scalar.activation(y[:, :], bank[L1_BANK][:, :], ACT.Copy).then_inc(ha_copied, 1)

                def exp(g):
                    if g == 0:
                        act.wait_ge(key_bias_done, T * (i + 1))
                    act.wait_ge(score_psum, G * i + g + 1)
                    for kt in range(NT):
                        nc.scalar.activation(w[:, g, kt, :], bank[L0_BANK + g][:, kt * nodes:(kt + 1) * nodes], ACT.Exp,
                                             bias=key_bias[:, NT * g + kt:NT * g + kt + 1]).then_inc(exp_done, 1)

                def high_z(t):
                    high(kz_h[:, t, :], bank[L1_BANK + t % 2][:, :], z_psum, T * j + t + 1, z_high)

                def high_v(t):
                    high(v_h[:, t, :], bank[L0_BANK + (t + 2) % 4][:, :], v_psum, T * i + t + 1, v_high)

                def high_w(g):
                    act.wait_ge(w_done, G * i + g + 1)
                    nc.scalar.activation(w_h[:, g], w[:, g], ACT.Copy).then_inc(w_high, 1)

                if layer0:
                    if layer1:
                        act.wait_ge(key_bias_done, T * (i + 1))
                        relu_norm(1, x1, j, 0)
                        relu_norm(1, x1, j, 1)
                    high_kp(0)
                    high_kp(1)
                    if layer1:
                        relu_norm(1, x1, j, 2)
                        relu_norm(1, x1, j, 3)
                    high_kp(2)
                    high_kp(3)
                    if layer1:
                        high_gT(j, 0)
                        high_gT(j, 1)
                    else:
                        high_weight(2)
                        act.wait_ge(weight_split, 3)
                    exp(0)
                    if layer1:
                        high_gT(j, 2)
                        high_gT(j, 3)
                    exp(1)
                    high_w(0)
                    high_w(1)
                if layer1:
                    high_z(0)
                    high_z(1)
                else:
                    high_v(0)
                if more:
                    relu_norm(0, x_in, i + 1, 0)
                    relu_norm(0, x_in, i + 1, 1)
                if layer1:
                    high_z(2)
                else:
                    high_v(1)
                if layer0:
                    act.wait_ge(w_summed, G * (i + 1))
                    nc.scalar.activation(sum_h[:, :, :], w[:, :, 0, :], ACT.Copy).then_inc(sum_high, 1)
                if more:
                    relu_norm(0, x_in, i + 1, 2)
                    relu_norm(0, x_in, i + 1, 3)
                if not layer1:
                    high_weight(3)
                if layer1:
                    high_z(3)
                if layer0:
                    if layer1:
                        high_v(0)
                        high_v(1)
                    high_v(2)
                    high_v(3)
                if more:
                    for t in range(T):
                        if layer1:
                            copy_ha(t)
                        high_hT(i + 1, t)
                elif layer0:
                    copy_ha(0)
                    for t in range(T):
                        relu_norm(1, x_in, i, t)
                    copy_ha(1)
                    high_gT(i, 0, hT_h)
                    high_gT(i, 1, hT_h)
                    copy_ha(2)
                    high_gT(i, 2, hT_h)
                    high_gT(i, 3, hT_h)
                    copy_ha(3)
                else:
                    for t in range(T):
                        copy_ha(t)
                if layer0:
                    act.wait_ge(adjT_loaded, 16 * (i + 1))
                    if layer1:
                        act.wait_ge(az_psum, T * (j + 1))
                    nc.scalar.activation(at_h[:, :, :], adjT[:, :, :], ACT.Copy).then_inc(at_high, 1)

            steps(act, step)

        @block.vector
        def _(dve):
            def low(dst, src, high_part, high_done, count, done):
                dve.wait_ge(high_done, count)
                nc.vector.tensor_tensor(dst, src, high_part.bitcast(F32), ALU.subtract).then_inc(done, 1)

            def low_hT(i, dt):
                dve.wait_ge(hT_high, DT * i + dt + 1)
                nc.vector.scalar_tensor_tensor(out=hT_l[:, dt, :], in0=xT[:, dt, :], scalar=0.0,
                                               in1=hT_h[:, dt, :].bitcast(F32), op0=ALU.max,
                                               op1=ALU.subtract).then_inc(hT_split, 1)

            def tile_stats(n, src, t):
                nc.vector.bn_stats(stats[n][:, t, :], src[:, t, :]).then_inc(stats_done[n], 1)

            def moments(n, i, g):
                tiles = slice(NT * g, NT * g + NT)
                dve.wait_ge(stats_done[n], T * i + NT * (g + 1))
                nc.vector.tensor_tensor(mean_sum[n][:, tiles], stats[n][:, tiles, 1], stats[n][:, tiles, 4],
                                        ALU.add).then_inc(moments_done[n], 1)
                for t in range(NT * g, NT * g + NT):
                    nc.vector.bn_aggr(mean_var[n][:, t, :], stats[n][:, t, :]).then_inc(aggr_done[n], 1)
                dve.wait_ge(aggr_done[n], T * i + NT * (g + 1))
                nc.vector.tensor_scalar(var_eps[n][:, tiles], mean_var[n][:, tiles, 1], LN_EPS, None,
                                        ALU.add).then_inc(moments_done[n], 1)

            def layer0_stats(i, g):
                dve.wait_ge(x_loaded, 16 * (i + 1))
                for t in range(NT * g, NT * (g + 1)):
                    tile_stats(0, x_in, t)
                moments(0, i, g)

            def degrees(i):
                dve.wait_ge(adj_loaded, 16 * (i + 1))
                nc.vector.tensor_reduce(deg[:, :], adj_in, AX_X, ALU.add).then_inc(deg_done, 1)
                dve.wait_ge(deg_done, 3 * i + 1)
                nc.vector.tensor_scalar(deg[:, :], deg[:, :], DEG_EPS, None, ALU.max).then_inc(deg_done, 1)
                dve.wait_ge(deg_done, 3 * i + 2)
                nc.vector.reciprocal(deg_inv[:, :], deg[:, :]).then_inc(deg_done, 1)

            def key_biases(i, g, ahead=True):
                dve.wait_ge(h_done[0], T * i + NT * (g + 1))
                if ahead and g == 0:
                    dve.wait_ge(exp_done, T * i)
                for t in range(NT * g, NT * (g + 1)):
                    nc.vector.tensor_tensor_reduce(h[:, t, :], h[:, t, :], u_b[:, :], 1.0, bqk[:, 0:1],
                                                   ALU.mult, ALU.add, key_bias[:, t:t + 1]).then_inc(key_bias_done, 1)

            for g in range(G):
                layer0_stats(0, g)
            dve.wait_ge(bias_loaded, 32)
            for o in range(DT):
                dve.wait_ge(wqk_loaded[o], 32)
                for k, (rows, bias) in enumerate(((xb, bq_c), (x1, bk_c))):
                    if o == 0:
                        nc.vector.tensor_scalar(wb_parts[:, k, :], rows[:, o, :], bias[:, o:o + 1], None,
                                                ALU.mult).then_inc(parts_done, 1)
                    else:
                        dve.wait_ge(parts_done, 2 * o - 1 + k)
                        nc.vector.scalar_tensor_tensor(out=wb_parts[:, k, :], in0=rows[:, o, :], scalar=bias[:, o:o + 1],
                                                       in1=wb_parts[:, k, :], op0=ALU.mult,
                                                       op1=ALU.add).then_inc(parts_done, 1)
            nc.vector.tensor_tensor_reduce(sum_inv[:, :], bq_c[:, :], bk_c[:, :], 1.0, 0.0, ALU.mult, ALU.add,
                                           sums[:, 0:1]).then_inc(parts_done, 1)
            for t in range(DT):
                low(n_l[:, t, :], bank[t][:, :], n_h[:, t, :], n_high, t + 1, n_split)
            for dt in range(DT):
                low(hT_l[:, dt, :], bank[TR_BANK + dt % 2][:, :], hT_h[:, dt, :], hT_high, dt + 1, hT_split)
            dve.wait_ge(setup_psum, DT + 1)
            dve.wait_ge(diagonal_done, 1)
            nc.vector.tensor_copy(u_b[:, :], bank[5][:, :]).then_inc(u_done, 1)

            def low_weight(n):
                (hi, lo), tiles, _, place = weight_pieces[n]
                low(lo[:, tiles, :], place, hi[:, tiles, :], weight_high, n + 1, weight_split)

            low_weight(0)
            low_weight(1)
            dve.wait_ge(setup_psum, DT + 2)
            nc.vector.tensor_copy(kp_bias[:, :], bank[4][:, 0:DT]).then_inc(bias_columns_done, 1)
            nc.vector.tensor_copy(bqk[:, :], bank[4][:, DT:DT + 1]).then_inc(bias_columns_done, 1)
            dve.wait_ge(bias_columns_done, 2)
            dve.wait_ge(u_done, 1)

            def step(i, layer0=True, layer1=True, more=True):
                j = i - 1
                first = isinstance(i, int) and i == 1

                def low_kp(dt):
                    dve.wait_ge(kp_high, DT * i + dt + 1)
                    nc.vector.scalar_tensor_tensor(out=kz_l[:, dt, :], in0=bank[L0_BANK + (dt + 2) % 4][:, :],
                                                   scalar=kp_bias[:, dt:dt + 1], in1=kz_h[:, dt, :].bitcast(F32),
                                                   op0=ALU.add, op1=ALU.subtract).then_inc(kp_split, 1)

                def low_gT(j, dt, hi=gT_h, lo=gT_l):
                    low(lo[:, dt, :], bank[TR_BANK + dt % 2][:, :], hi[:, dt, :], gT_high, DT * j + dt + 1, gT_split)

                def weigh(g):
                    if g == 0:
                        dve.wait_ge(adjT_loaded, 16 * (i + 1))
                    dve.wait_ge(exp_done, T * i + NT * (g + 1))
                    nc.vector.tensor_tensor(w[:, g], w[:, g], adjT[:, NT * g:NT * (g + 1), :], ALU.mult).then_inc(w_done, 1)

                def low_z(t):
                    low(kz_l[:, t, :], bank[L1_BANK + t % 2][:, :], kz_h[:, t, :], z_high, T * j + t + 1, z_split)

                def low_v(t):
                    low(v_l[:, t, :], bank[L0_BANK + (t + 2) % 4][:, :], v_h[:, t, :], v_high, T * i + t + 1, v_split)

                def layer1_result(t):
                    dve.wait_ge(az_psum, T * j + t + 1)
                    dve.wait_ge(ha_copied, T * j + t + 1)
                    nc.vector.scalar_tensor_tensor(out=y[:, :], in0=bank[L1_BANK + 1][:, :],
                                                   scalar=deg_inv[:, t:t + 1], in1=y[:, :],
                                                   op0=ALU.mult, op1=ALU.add).then_inc(y_done, 1)
                    dve.wait_ge(y_done, T * j + t + 1)
                    place = (x1 if layer0 else x_in)[:, t, :]
                    nc.vector.scalar_tensor_tensor(out=place, in0=y[:, :], scalar=0.0, in1=place,
                                                   op0=ALU.max, op1=ALU.add).then_inc(x2_done, 1)

                def layer0_result(t):
                    dst = x1 if more else x_in
                    dve.wait_ge(xb_done, T * i + t + 1)
                    dve.wait_ge(av_psum, T * i + t + 1)
                    if layer1 and more:
                        dve.wait_ge(out_stored[t], 16 * (j + 1))
                    nc.vector.scalar_tensor_tensor(out=dst[:, t, :], in0=bank[L0_BANK + (t + 2) % 4][:, :],
                                                   scalar=sum_inv[:, t:t + 1], in1=xb[:, t, :],
                                                   op0=ALU.mult, op1=ALU.add).then_inc(x1_done, 1)

                def layer1_stats(t):
                    dve.wait_ge(x1_done, T * i + t + 1)
                    tile_stats(1, x1 if more else x_in, t)

                def sum_inverses():
                    dve.wait_ge(key_bias_done, T * (i + 2) if more else T * (i + 1))
                    dve.wait_ge(sum_psum, i + 1)
                    own = h[:, 0, :].rearrange("p (t n) -> p t n", t=T)
                    every = bank[TR_BANK][:, :].rearrange("p (t n) -> p t n", t=T)
                    mask = diagonal[:, :].rearrange("p (a n) -> p a n", a=1).to_broadcast([P, T, P])
                    nc.vector.tensor_tensor(own.bitcast(I32), every.bitcast(I32), mask,
                                            ALU.bitwise_and).then_inc(sum_taken, 1)
                    dve.wait_ge(sum_taken, 2 * i + 1)
                    nc.vector.tensor_reduce(sums[:, :], own, AX_X, ALU.add).then_inc(sum_taken, 1)
                    dve.wait_ge(sum_taken, 2 * i + 2)
                    nc.vector.reciprocal(sum_inv[:, :], sums[:, :]).then_inc(sum_inv_done, 1)
                    dve.wait_ge(sum_inv_done, i + 1)

                if layer0:
                    low_kp(0)
                    low_kp(1)
                    if layer1:
                        degrees(j)
                    else:
                        layer0_stats(1, 0)
                    low_kp(2)
                    if not layer1:
                        layer0_stats(1, 1)
                    low_kp(3)
                    if layer1:
                        low_gT(j, 0)
                        low_gT(j, 1)
                    else:
                        low_weight(2)
                        key_biases(0, 0, ahead=False)
                        key_biases(0, 1)
                    weigh(0)
                    if layer1:
                        low_gT(j, 2)
                        low_gT(j, 3)
                    weigh(1)
                    if not layer1:
                        for g in range(G):
                            split_w(dve, 0, g)
                if layer1 and more:
                    layer0_stats(i + 1, 0)
                if layer1:
                    low_z(0)
                if layer1 and more:
                    layer0_stats(i + 1, 1)
                if layer1:
                    low_z(1)
                    low_z(2)
                    low_z(3)
                    if not layer0:
                        degrees(j)
                if layer0:
                    low_v(0)
                    low_v(1)
                if more:
                    key_biases(i + 1, 0)
                    key_biases(i + 1, 1)
                if not layer1:
                    low_weight(3)
                if layer0:
                    low_v(2)
                    low_v(3)
                if layer1:
                    dve.wait_ge(deg_done, 3 * (j + 1))
                if more and layer1:
                    for t in range(T):
                        layer1_result(t)
                        low_hT(i + 1, t)
                if layer0:
                    if not layer1:
                        for t in range(T - 1):
                            low_hT(1, t)
                    sum_inverses()
                    if not layer1:
                        low_hT(1, T - 1)
                    layer0_result(0)
                    layer1_stats(0)
                    layer0_result(1)
                    layer0_result(2)
                    layer1_stats(1)
                    moments(1, i, 0)
                    layer0_result(3)
                    layer1_stats(2)
                    layer1_stats(3)
                    moments(1, i, 1)
                if not more:
                    layer1_result(0)
                    layer1_result(1)
                    if layer0:
                        low_gT(i, 0, hT_h, hT_l)
                        low_gT(i, 1, hT_h, hT_l)
                    layer1_result(2)
                    if layer0:
                        low_gT(i, 2, hT_h, hT_l)
                        low_gT(i, 3, hT_h, hT_l)
                    layer1_result(3)

            steps(dve, step)


_OUT = (64, 256, 512)


def kernel(**inputs):
    import numpy as _np
    import concourse.bacc as _bacc
    from concourse.bass_utils import run_bass_kernel_spmd as _run

    arrays = {
        "x": inputs["x"], "x_t": _np.swapaxes(inputs["x"], 1, 2), "adj": inputs["adj"], "adj_t": _np.swapaxes(inputs["adj"], 1, 2),
        "wq": inputs["L0_gnn_Wq_w"], "bq": inputs["L0_gnn_Wq_b"],
        "wk": inputs["L0_gnn_Wk_w"], "bk": inputs["L0_gnn_Wk_b"],
        "wv_t": _np.transpose(inputs["L0_gnn_Wv_w"]), "bv": inputs["L0_gnn_Wv_b"],
        "w1_t": _np.transpose(inputs["L1_gnn_W"]),
    }
    arrays = {name: _np.ascontiguousarray(a) for name, a in arrays.items()}
    nc = _bacc.Bacc("TRN2", target_bir_lowering=False, num_devices=1)
    args = [nc.dram_tensor(name, a.shape, F32, kind="ExternalInput").ap() for name, a in arrays.items()]
    out = nc.dram_tensor("out", _OUT, F32, kind="ExternalOutput").ap()
    gnn_layers(nc, *args, out)
    r = _run(nc, [arrays], core_ids=[0])
    return r.results[0]["out"]
```
